# Optimizing a Trainium2 kernel written in Bass

```python
import numpy as np
import jax
import jax.numpy as jnp

def _softmax(x, axis=-1):
    return jax.nn.softmax(x, axis=axis)

def _gelu(x):
    return jax.nn.gelu(x, approximate=True)

def _silu(x):
    return jax.nn.silu(x)

def _sigmoid(x):
    return jax.nn.sigmoid(x)

def _layernorm(x, axis=-1, eps=1e-05):
    m = jnp.mean(x, axis=axis, keepdims=True)
    v = jnp.var(x, axis=axis, keepdims=True)
    return (x - m) / jnp.sqrt(v + eps)

def _scatter_add(tgt, idx, src, axis=0):
    return tgt.at[idx].add(src)

def _segment_sum(src, seg, n):
    return jax.ops.segment_sum(src, seg, n)
kernel_name = 'mk_xattn_seq_d1_seqx_r2_ee4a18'

def setup_inputs(seed: int=0):
    np.random.seed(seed)
    _w = jnp.asarray

    def _rec_inputs():
        import jax
        import jax.numpy as jnp
        _rk = jax.random.key(seed)
        x = 7.22e-05 + 1 * jax.random.normal(jax.random.fold_in(_rk, 1), (32, 512, 512), jnp.float32)
        _lenS = 512 - jax.random.randint(jax.random.fold_in(_rk, 7), (32,), 0, max(1, 512 // 4) + 1, jnp.int32)
        _lenS2 = 77 - jax.random.randint(jax.random.fold_in(_rk, 8), (32,), 0, max(1, 77 // 4) + 1, jnp.int32)
        _ctx_1024P = jax.random.normal(jax.random.fold_in(_rk, 11), (32, 16, 512), jnp.float32)
        _ctx_1024c = jax.random.dirichlet(jax.random.fold_in(_rk, 511), 0.3 * jnp.ones((16,), jnp.float32), (32, 77))
        _ctx_1024t = jnp.einsum('bsk,bkd->bsd', _ctx_1024c, _ctx_1024P)
        _ctx_1024t = _ctx_1024t * jax.lax.rsqrt(jnp.mean(jnp.square(_ctx_1024t)) + 1e-12) * 0.953939
        ctx_1024 = 4.13588e-05 + 0.999923 * (_ctx_1024t + 0.3 * jax.random.normal(jax.random.fold_in(_rk, 611), (32, 77, 512), jnp.float32))
        return (x, ctx_1024)
    x, ctx_1024 = _rec_inputs()

    def _L0_xattn_setup():
        import jax, jax.numpy as jnp
        import numpy as np
        EPS = 1e-06
        ROPE_BASE = 10000.0

        def rmsnorm(x, w):
            return x * jax.lax.rsqrt(jnp.mean(x * x, axis=-1, keepdims=True) + EPS) * w

        def rope(t, offset, head_dim):
            T = t.shape[1]
            half = head_dim // 2
            inv_freq = 1.0 / ROPE_BASE ** (jnp.arange(0, half, dtype=jnp.float32) / half)
            pos = jnp.arange(T, dtype=jnp.float32) + offset
            ang = pos[:, None] * inv_freq[None, :]
            cos = jnp.concatenate([jnp.cos(ang), jnp.cos(ang)], axis=-1)[None, :, None, :]
            sin = jnp.concatenate([jnp.sin(ang), jnp.sin(ang)], axis=-1)[None, :, None, :]
            t1, t2 = (t[..., :half], t[..., half:])
            rot = jnp.concatenate([-t2, t1], axis=-1)
            return t * cos + rot * sin
        key = jax.random.key(seed)
        ks = jax.random.split(key, 6)
        B, Td, Te, d = (4, 1024, 1024, 512)
        s = 1.0 / np.sqrt(d)
        return {'x': jax.random.normal(ks[0], (B, Td, d), jnp.float32), 'encoder_out': jax.random.normal(ks[1], (B, Te, d), jnp.float32), 'norm_w': jnp.ones((d,), jnp.float32), 'Wq': jax.random.normal(ks[2], (d, d), jnp.float32) * s, 'Wkv': jax.random.normal(ks[3], (2 * d, d), jnp.float32) * s, 'Wo': jax.random.normal(ks[4], (d, d), jnp.float32) * s, 'decoder_offset': 0}
    _L0_xattn_all = _L0_xattn_setup()
    _L0_xattn_in = {k: v for k, v in _L0_xattn_all.items() if k in ('norm_w', 'Wq', 'Wkv', 'Wo')}
    del _L0_xattn_all
    return {'x': x, 'ctx_1024': ctx_1024, 'L0_xattn_norm_w': _L0_xattn_in['norm_w'], 'L0_xattn_Wq': _L0_xattn_in['Wq'], 'L0_xattn_Wkv': _L0_xattn_in['Wkv'], 'L0_xattn_Wo': _L0_xattn_in['Wo']}

def reference(x, ctx_1024, L0_xattn_norm_w, L0_xattn_Wq, L0_xattn_Wkv, L0_xattn_Wo):
    import jax
    import jax.numpy as jnp

    def _L0_xattn_ref(x, encoder_out, norm_w, Wq, Wkv, Wo, decoder_offset):
        import jax, jax.numpy as jnp
        import numpy as np
        EPS = 1e-06
        ROPE_BASE = 10000.0

        def rmsnorm(x, w):
            return x * jax.lax.rsqrt(jnp.mean(x * x, axis=-1, keepdims=True) + EPS) * w

        def rope(t, offset, head_dim):
            T = t.shape[1]
            half = head_dim // 2
            inv_freq = 1.0 / ROPE_BASE ** (jnp.arange(0, half, dtype=jnp.float32) / half)
            pos = jnp.arange(T, dtype=jnp.float32) + offset
            ang = pos[:, None] * inv_freq[None, :]
            cos = jnp.concatenate([jnp.cos(ang), jnp.cos(ang)], axis=-1)[None, :, None, :]
            sin = jnp.concatenate([jnp.sin(ang), jnp.sin(ang)], axis=-1)[None, :, None, :]
            t1, t2 = (t[..., :half], t[..., half:])
            rot = jnp.concatenate([-t2, t1], axis=-1)
            return t * cos + rot * sin
        B, Td, d = x.shape
        Te = encoder_out.shape[1]
        H = 16
        D = d // H
        residual = x
        h = rmsnorm(x, norm_w)
        q = (h @ Wq.T).reshape(B, Td, H, D)
        kv = (encoder_out @ Wkv.T).reshape(B, Te, 2, H, D)
        k, v = (kv[:, :, 0], kv[:, :, 1])
        q = rope(q, decoder_offset, D)
        k = rope(k, 0, D)
        scale = 1.0 / np.sqrt(D)
        scores = jnp.einsum('bqhd,bkhd->bhqk', q, k) * scale
        attn = jax.nn.softmax(scores, axis=-1)
        out = jnp.einsum('bhqk,bkhd->bqhd', attn, v).reshape(B, Td, d)
        out = out @ Wo.T
        return residual + out
    x = _L0_xattn_ref(x, ctx_1024, L0_xattn_norm_w, L0_xattn_Wq, L0_xattn_Wkv, L0_xattn_Wo, 0)
    return x

_drawn_inputs = setup_inputs


def setup_inputs(seed=0):
    import zlib

    import numpy as np

    out = dict(_drawn_inputs(seed))
    spreads = {'L0_xattn_norm_w': (1.0, 0.2)}
    factors = {}
    for name, (base, spread) in spreads.items():
        noise = np.random.default_rng([zlib.crc32(name.encode()), seed]).standard_normal(out[name].shape)
        drawn = base * np.exp(spread * noise) if base else spread * noise
        out[name] = jnp.asarray(drawn.astype(out[name].dtype))
    for name, factor in factors.items():
        out[name] = (out[name] * factor).astype(out[name].dtype)
    return out
```

```python
from contextlib import ExitStack

import concourse.bass as bass
from concourse import mybir

F32 = mybir.dt.float32
F16 = mybir.dt.float16
ALU = mybir.AluOpType
ACT = mybir.ActivationFunctionType
AX = mybir.AxisListType
ABSMAX = bass.bass_isa.ReduceOp.absmax

P = 128
B, T, D = 32, 512, 512
S = 77
H, HD = 16, 32
KT = D // P
TT = T // P
G = H * HD // P
J = P // HD
UNITS = B * G
NTOK = B * S
CT = (NTOK + P - 1) // P
KCHUNK = (T // S) * S
EPS = 1e-6
TINY = 1e-30

W_TOP = 64.0
H_GAIN = 64.0
Q_GAIN = 1.0 / (W_TOP * H_GAIN)
K_TOP = 2.0
O_TOP = 256.0

STACK = 3 * HD + 2
SWAP = [(d + HD // 2) % HD for d in range(HD)]

C_ID, C_COSQ, C_SINQ = 0, P, P + T
C_COSK, C_SINK = P + 2 * T, P + 2 * T + S
C_SEL = P + 2 * T + 2 * S
C_ONES = C_SEL + G * P
C_END = C_ONES + G * HD


def shape_constants():
    import numpy as np

    c = np.zeros((P, C_END), np.float32)
    c[:, C_ID:C_ID + P] = np.eye(P, dtype=np.float32)
    half = HD // 2
    freq = (np.float32(1.0) / np.float32(10000.0) ** (np.arange(half, dtype=np.float32) / np.float32(half)))
    feature = np.arange(P) % HD
    sign = np.where(feature < half, -1.0, 1.0).astype(np.float32)[:, None]
    column = np.arange(T)
    q_pos = (TT * (column % P) + column // P).astype(np.float32)
    q_ang = freq.astype(np.float32)[feature % half][:, None] * q_pos[None, :]
    k_ang = freq.astype(np.float32)[feature % half][:, None] * np.arange(S, dtype=np.float32)[None, :]
    c[:, C_COSQ:C_COSQ + T] = np.cos(q_ang) * np.float32(Q_GAIN)
    c[:, C_SINQ:C_SINQ + T] = np.sin(q_ang) * sign * np.float32(Q_GAIN)
    c[:, C_COSK:C_COSK + S] = np.cos(k_ang)
    c[:, C_SINK:C_SINK + S] = np.sin(k_ang) * sign
    for g in range(G):
        for j in range(J):
            c[HD * j + (HD // G) * g, C_SEL + g * P + HD * j:C_SEL + g * P + HD * (j + 1)] = 1.0
        c[:S, C_ONES + g * HD + (HD // G) * g:C_ONES + g * HD + (HD // G) * (g + 1)] = 1.0 / O_TOP
    return c


def wait_from_first(eng, sem, value):
    if not isinstance(value, int) or value > 0:
        eng.wait_ge(sem, value)


def setup_block(nc, sb_keep, x_ctx, norm_w, w_q, w_kv, w_o, consts_in, k_hi_dram, k_lo_dram, v_dram):
    consts, wq, wo, sel16, scales = sb_keep
    ident = consts[:, C_ID:C_ID + P]
    mats = [w_kv[0:D, :], w_kv[D:2 * D, :], w_q, w_o]
    W_ITEMS = len(mats) * KT
    ITEMS = W_ITEMS + CT
    chunks = [(c, min(KCHUNK, NTOK - c)) for c in range(0, NTOK, KCHUNK)]
    k_items = [(c, n, m) for c, n in chunks for m in range(G)]
    order = []
    for n in range(max(len(k_items), CT)):
        if n < len(k_items):
            order.append(("k", n))
        if n < CT:
            order.append(("v", n))
    CRING = 8

    def tokens(t):
        return min(P, NTOK - t * P)

    with ExitStack() as ctx:
        sb = lambda name, shape, dt=F32: ctx.enter_context(nc.sbuf_tensor(name, shape, dt))
        sem = lambda name: ctx.enter_context(nc.semaphore(name))
        w_nat = sb("w_nat", [P, 2, KT, D])
        w_t = sb("w_t", [P, len(mats), KT, D])
        w_col = sb("w_col", [P, KT])
        c_nat = sb("c_nat", [P, CRING, D])
        c_t = sb("c_t", [P, KT, NTOK])
        k_rot = sb("k_rot", [P, G, NTOK])
        k_hi = sb("k_hi", [P, NTOK], F16)
        k_lo = sb("k_lo", [P, NTOK], F16)
        v_row = sb("v_row", [P, 2, D])
        swapped = sb("k_swapped", [P, KCHUNK])
        cos_part = sb("k_cos_part", [P, KCHUNK])
        sin_part = sb("k_sin_part", [P, KCHUNK])
        peak = sb("peak", [P, len(k_items) + CT])
        tops = sb("tops", [P, 4])
        top_all = sb("top_all", [P, 4])
        inv = sb("inv", [P, 4])
        gain = sb("gain", [P, 4])
        tp = ctx.enter_context(nc.psum_tensor("tp", [P, 4, D], F32))
        kp = ctx.enter_context(nc.psum_tensor("kp", [P, 2, D], F32))
        vp = ctx.enter_context(nc.psum_tensor("vp", [P, 2, D], F32))

        const_in = sem("const_in")
        w_in = [sem(f"w_in{n}") for n in range(2)]
        c_in = [sem(f"c_in{n}") for n in range(CRING)]
        turned = sem("set_turned")
        copied_a = sem("copied_a")
        copied_v = sem("copied_v")
        k_done = sem("k_done")
        v_done = sem("v_done")
        k_read = sem("k_read")
        k_sin = sem("k_sin")
        k_full = sem("k_full")
        k_peak = sem("k_peak")
        v_copied = sem("v_copied")
        v_peaked = sem("v_peaked")
        v_out = [sem(f"v_out{n}") for n in range(2)]
        top_in = sem("top_in")
        top_out = sem("top_out")
        gained = sem("gained")
        step = sem("step")
        split_hi = sem("split_hi")
        split_lo = sem("split_lo")
        k_out = sem("k_out")
        sel_done = sem("sel_done")

        block = ctx.enter_context(nc.Block())

        @block.sync
        def _(sp):
            sp.dma_start(consts[:, :], consts_in).then_inc(const_in, 16)
            sp.dma_start(w_col[:, :], norm_w.rearrange("(k p) -> p k", p=P), allow_slow_non_contiguous=True).then_inc(const_in, 16)
            for m, w in enumerate(mats):
                if m >= 2:
                    sp.wait_ge(turned, KT * (m - 1))
                sp.dma_start(w_nat[:, m % 2, :, :], w.rearrange("(t p) d -> p t d", p=P)).then_inc(w_in[m % 2], 16)
            for t in range(CT):
                n = tokens(t)
                if t >= CRING:
                    sp.wait_ge(turned, W_ITEMS + t - CRING + 1)
                sp.dma_start(c_nat[0:n, t % CRING, :], x_ctx[t * P:t * P + n, :]).then_inc(c_in[t % CRING], 16)
            for t in range(CT):
                n = tokens(t)
                sp.wait_ge(v_copied, t + 1)
                sp.dma_start(v_dram[t * P:t * P + n, :], v_row[0:n, t % 2, :]).then_inc(v_out[t % 2], 16)
            for m in range(G):
                rows = slice(m * P, (m + 1) * P)
                sp.wait_ge(split_hi, 3 + m)
                sp.dma_start(k_hi_dram[rows, :], k_hi[:, :]).then_inc(k_out, 16)
                sp.wait_ge(split_lo, 3 + m)
                sp.dma_start(k_lo_dram[rows, :], k_lo[:, :]).then_inc(k_out, 16)
            sp.wait_ge(k_out, 16 * 2 * G)
            for n in range(2):
                sp.wait_ge(v_out[n], 16 * ((CT + 1 - n) // 2))

        @block.tensor
        def _(pe):
            pe.wait_ge(const_in, 32)
            for item in range(ITEMS):
                if item >= 4:
                    pe.wait_ge(copied_v if item % 2 else copied_a, (item - 4) // 2 + 1)
                if item < W_ITEMS:
                    m, k = divmod(item, KT)
                    pe.wait_ge(w_in[m % 2], 16 * (m // 2 + 1))
                    for t in range(KT):
                        mm = nc.tensor.transpose(tp[:, item % 4, t * P:(t + 1) * P],
                                                 w_nat[:, m % 2, t, k * P:(k + 1) * P], ident)
                else:
                    t = item - W_ITEMS
                    n = tokens(t)
                    pe.wait_ge(c_in[t % CRING], 16 * (t // CRING + 1))
                    for k in range(KT):
                        mm = nc.tensor.transpose(tp[:, item % 4, k * P:k * P + n],
                                                 c_nat[0:n, t % CRING, k * P:(k + 1) * P], ident[0:n, 0:n])
                mm.then_inc(turned, 1)
            pe.wait_ge(copied_a, ITEMS // 2)
            pe.wait_ge(copied_v, ITEMS // 2)
            for kind, n in order:
                if kind == "k":
                    c, cols, m = k_items[n]
                    if n >= 2:
                        pe.wait_ge(k_read, n - 1)
                    for k in range(KT):
                        mm = nc.tensor.matmul(kp[:, n % 2, 0:cols], w_t[:, 0, k, m * P:(m + 1) * P],
                                              c_t[:, k, c:c + cols], start=(k == 0), stop=(k == KT - 1))
                    mm.then_inc(k_done, 1)
                else:
                    rows = tokens(n)
                    if n >= 2:
                        pe.wait_ge(v_copied, n - 1)
                        pe.wait_ge(v_peaked, n - 1)
                    for k in range(KT):
                        mm = nc.tensor.matmul(vp[0:rows, n % 2, :], c_t[:, k, n * P:n * P + rows],
                                              w_t[:, 1, k, :], start=(k == 0), stop=(k == KT - 1))
                    mm.then_inc(v_done, 1)

        def copy_item(eng, item):
            src = tp[:, item % 4, :]
            if item < W_ITEMS:
                m, k = divmod(item, KT)
                dst, scale = w_t[:, m, k, :], (w_col[:, k:k + 1] if m == 2 else None)
            else:
                t = item - W_ITEMS
                n = tokens(t)
                src = src.rearrange("p (k n) -> p k n", k=KT)[:, :, 0:n]
                dst, scale = c_t[:, :, t * P:t * P + n], None
            if eng == "act":
                return nc.scalar.activation(dst, src, ACT.Copy, scale=1.0 if scale is None else scale)
            if scale is None:
                return nc.vector.tensor_copy(dst, src)
            return nc.vector.tensor_scalar(dst, src, scale, None, ALU.mult)

        @block.scalar
        def _(act):
            act.wait_ge(const_in, 32)
            for item in range(0, ITEMS, 2):
                act.wait_ge(turned, item + 1)
                copy_item("act", item).then_inc(copied_a, 1)
            for n in range(CT):
                rows = tokens(n)
                act.wait_ge(v_done, n + 1)
                if n >= 2:
                    act.wait_ge(v_out[n % 2], 16 * (n // 2))
                act.wait_ge(v_peaked, n + 1)
                nc.scalar.activation(v_row[0:rows, n % 2, :], vp[0:rows, n % 2, :], ACT.Copy).then_inc(v_copied, 1)
            for m, w in enumerate((wq, wo)):
                act.wait_ge(gained, m + 1)
                nc.scalar.activation(w[:, 0, :, :], w_t[:, 2 + m, :, :], ACT.Copy,
                                     scale=gain[:, m:m + 1]).then_inc(split_hi, 1)
            act.wait_ge(gained, 3)
            for m in range(G):
                if m >= 1:
                    act.wait_ge(split_lo, 2 + m)
                    act.wait_ge(k_out, 32 * m)
                nc.scalar.activation(k_hi[:, :], k_rot[:, m, :], ACT.Copy, scale=gain[:, 2:3]).then_inc(split_hi, 1)

        @block.gpsimd
        def _(pool):
            for n, (c, cols, m) in enumerate(k_items):
                reps = cols // S
                pool.wait_ge(k_read, n + 1)
                if n >= 1:
                    pool.wait_ge(k_full, n)
                nc.gpsimd.tensor_tensor(
                    sin_part[:, 0:cols].rearrange("p (b s) -> p b s", s=S),
                    swapped[:, 0:cols].rearrange("p (b s) -> p b s", s=S),
                    consts[:, C_SINK:C_SINK + S].unsqueeze(1).to_broadcast([P, reps, S]), ALU.mult).then_inc(k_sin, 1)
            for n in range(4):
                pool.wait_ge(top_in, n + 1)
                nc.gpsimd.partition_all_reduce(top_all[:, n:n + 1], tops[:, n:n + 1], P, ABSMAX).then_inc(top_out, 1)

        @block.vector
        def _(dve):
            done = [0]

            def link(instruction):
                done[0] += 1
                instruction.then_inc(step, 1)
                dve.wait_ge(step, done[0])

            dve.wait_ge(const_in, 32)
            nc.vector.tensor_copy(sel16[:, :], consts[:, C_SEL:C_SEL + G * P]).then_inc(sel_done, 1)
            for item in range(1, ITEMS, 2):
                dve.wait_ge(turned, item + 1)
                copy_item("dve", item).then_inc(copied_v, 1)
            dve.wait_ge(copied_a, W_ITEMS // 2)
            dve.wait_ge(copied_v, W_ITEMS // 2)
            for m in range(2):
                nc.vector.tensor_reduce(tops[:, m:m + 1], w_t[:, 2 + m, :, :], AX.XY, ALU.max, apply_absolute_value=True).then_inc(top_in, 1)
            for kind, n in order:
                if kind == "k":
                    c, cols, m = k_items[n]
                    reps = cols // S
                    dve.wait_ge(k_done, n + 1)
                    if n >= 1:
                        dve.wait_ge(k_sin, n)
                        dve.wait_ge(k_full, n)
                    nc.vector.stream_shuffle(swapped[:, 0:cols], kp[:, n % 2, 0:cols], SWAP)
                    nc.vector.tensor_tensor(
                        cos_part[:, 0:cols].rearrange("p (b s) -> p b s", s=S),
                        kp[:, n % 2, 0:cols].rearrange("p (b s) -> p b s", s=S),
                        consts[:, C_COSK:C_COSK + S].unsqueeze(1).to_broadcast([P, reps, S]),
                        ALU.mult).then_inc(k_read, 1)
                    dve.wait_ge(k_read, n + 1)
                    dve.wait_ge(k_sin, n + 1)
                    nc.vector.tensor_tensor(k_rot[:, m, c:c + cols], cos_part[:, 0:cols], sin_part[:, 0:cols],
                                            ALU.add).then_inc(k_full, 1)
                    dve.wait_ge(k_full, n + 1)
                    nc.vector.tensor_reduce(peak[:, n:n + 1], k_rot[:, m, c:c + cols], AX.X,
                                            ALU.max, apply_absolute_value=True).then_inc(k_peak, 1)
                else:
                    rows = tokens(n)
                    if rows < P:
                        link(nc.vector.memset(peak[:, len(k_items) + n:len(k_items) + n + 1], 0.0))
                    dve.wait_ge(v_done, n + 1)
                    nc.vector.tensor_reduce(peak[0:rows, len(k_items) + n:len(k_items) + n + 1],
                                            vp[0:rows, n % 2, :], AX.X, ALU.max, apply_absolute_value=True).then_inc(v_peaked, 1)
            dve.wait_ge(k_peak, len(k_items))
            dve.wait_ge(v_peaked, CT)
            nc.vector.tensor_reduce(tops[:, 2:3], peak[:, 0:len(k_items)], AX.X, ALU.max).then_inc(top_in, 1)
            nc.vector.tensor_reduce(tops[:, 3:4], peak[:, len(k_items):len(k_items) + CT], AX.X, ALU.max).then_inc(top_in, 1)
            for n in range(4):
                dve.wait_ge(top_out, n + 1)
                link(nc.vector.tensor_scalar(top_all[:, n:n + 1], top_all[:, n:n + 1], TINY, None, ALU.max))
                link(nc.vector.reciprocal(inv[:, n:n + 1], top_all[:, n:n + 1]))
                nc.vector.tensor_scalar(gain[:, n:n + 1], inv[:, n:n + 1], (W_TOP, W_TOP, K_TOP, 1.0)[n], None,
                                        ALU.mult).then_inc(gained, 1)
            dve.wait_ge(gained, 4)
            nc.vector.tensor_scalar(scales[:, 0:1], top_all[:, 0:1], top_all[:, 2:3], HD ** -0.5 / K_TOP, ALU.mult, ALU.mult)
            nc.vector.tensor_copy(scales[:, 1:2], gain[:, 3:4])
            nc.vector.tensor_scalar(scales[:, 2:3], top_all[:, 1:2], top_all[:, 3:4], 1.0 / (W_TOP * O_TOP), ALU.mult, ALU.mult)
            for m, w in enumerate((wq, wo)):
                dve.wait_ge(split_hi, m + 1)
                nc.vector.scalar_tensor_tensor(out=w[:, 1, :, :], in0=w_t[:, 2 + m, :, :], scalar=gain[:, m:m + 1],
                                               in1=w[:, 0, :, :], op0=ALU.mult, op1=ALU.subtract).then_inc(split_lo, 1)
            for m in range(G):
                dve.wait_ge(split_hi, 3 + m)
                if m >= 1:
                    dve.wait_ge(k_out, 32 * m)
                nc.vector.scalar_tensor_tensor(out=k_lo[:, :], in0=k_rot[:, m, :], scalar=gain[:, 2:3],
                                               in1=k_hi[:, :], op0=ALU.mult, op1=ALU.subtract).then_inc(split_lo, 1)


def attention_block(nc, sb_keep, x, out, k_hi_dram, k_lo_dram, v_dram):
    consts, wq, wo, sel16, scales = sb_keep
    ident = consts[:, C_ID:C_ID + P]
    cos_q = consts[:, C_COSQ:C_COSQ + T]
    sin_q = consts[:, C_SINQ:C_SINQ + T]
    ones = consts[0:S, C_ONES:C_ONES + G * HD]
    exp_scale, v_scale, out_scale = scales[:, 0:1], scales[:, 1:2], scales[:, 2:3]

    x_load = x.rearrange("b (p j) d -> b p j d", j=TT)
    x_tile = x.rearrange("b (p j) d -> b j p d", j=TT)
    out_tile = out.rearrange("b (p j) d -> b j p d", j=TT)
    k_hi_heads = k_hi_dram.rearrange("(h d) (b s) -> b d h s", d=HD, s=S)
    k_lo_heads = k_lo_dram.rearrange("(h d) (b s) -> b d h s", d=HD, s=S)
    k_hi_groups = k_hi_dram.rearrange("(g j d) (b s) -> b j d g s", j=J, d=HD, s=S)
    v_batch = v_dram.rearrange("(b s) d -> b s d", s=S)

    FIRST, LAST = -3, B + 3
    LOOP_FROM, LOOP_TO = 4, B - 4

    with ExitStack() as ctx:
        sb = lambda name, shape, dt=F32: ctx.enter_context(nc.sbuf_tensor(name, shape, dt))
        ps = lambda name, shape: ctx.enter_context(nc.psum_tensor(name, shape, F32))
        sem = lambda name: ctx.enter_context(nc.semaphore(name))

        x_in = sb("x_in", [P, 2, TT, D])
        junk = sb("junk", [P, D], F16)
        sumsq = sb("sumsq", [P, TT])
        mean_eps = sb("mean_eps", [P, TT])
        scaled_eps = sb("scaled_eps", [P, 1])
        minus_half = sb("minus_half", [P, 1])
        rstd = sb("rstd", [P, TT])
        x_norm = sb("x_norm", [P, 2, TT, D])
        h_t = sb("h_t", [P, 2, 2, KT, T], F16)
        swapped = sb("swapped", [P, T])
        cos_part = sb("cos_part", [P, T])
        sin_part = sb("sin_part", [P, T])
        q_rot = sb("q_rot", [P, T])
        q_part = sb("q_part", [P, G, 2, T], F16)
        q_stack = sb("q_stack", [STACK, G, J, T], F16)
        k_stack = sb("k_stack", [STACK, 2, H, S], F16)
        k_diag = sb("k_diag", [P, 2, G, J * S], F16)
        v_sb = sb("v_sb", [S, 2, D])
        maxima = sb("maxima", [P, TT, J])
        max_part = sb("max_part", [P, TT, 2 * J], F16)
        max_row = sb("max_row", [2 * J, 2, T], F16)
        probs = sb("probs", [S, 2, J, T])
        o_raw = sb("o_raw", [P, 2, G, T])
        recip = sb("recip", [P, T])
        recip_part = sb("recip_part", [P, 2, T], F16)
        o_norm = sb("o_norm", [P, T])
        o_part = sb("o_part", [P, 2, 2, G, T], F16)
        res = sb("res", [P, TT, D])

        score_ps = ps("score_ps", [P, J, T])
        o_ps = ps("o_ps", [P, T])
        sum_ps = ps("sum_ps", [P, T])
        a_ps = ps("a_ps", [P, T])
        b_ps = ps("b_ps", [P, T])
        ident16 = sb("ident16", [P, P], F16)
        max_ps = a_ps[:, :].bitcast(F16)

        sp_passed = sem("sp_passed")
        zeroed = sem("zeroed")
        ready = sem("ready")
        x_got = [sem(f"x_got{n}") for n in range(2)]
        res_got = [sem(f"res_got{n}") for n in range(TT)]
        stored = [sem(f"stored{n}") for n in range(TT)]
        k_got = [sem(f"k_got{n}") for n in range(2)]
        diag_got = [sem(f"diag_got{n}") for n in range(2)]
        v_got = [sem(f"v_got{n}") for n in range(2)]
        stacked = [sem(f"stacked{n}") for n in range(2)]
        max_stacked = [sem(f"max_stacked{n}") for n in range(G)]
        squared, rstd_a, rstd_b, normed = sem("squared"), sem("rstd_a"), sem("rstd_b"), sem("normed")
        turned, h_hi, h_lo = sem("turned"), sem("h_hi"), sem("h_lo")
        q_done, q_read, q_sin, q_full, q_hi, q_lo = (sem(n) for n in ("q_done", "q_read", "q_sin", "q_full", "q_hi", "q_lo"))
        max_mm, max_red, max_hi, max_lo, max_t, max_rows = (
            sem(n) for n in ("max_mm", "max_red", "max_hi", "max_lo", "max_t", "max_rows"))
        scored, exped, valued, o_copied = (sem(n) for n in ("scored", "exped", "valued", "o_copied"))
        recip_done, recip_hi, recip_lo, spread = (sem(n) for n in ("recip_done", "recip_hi", "recip_lo", "spread"))
        o_full, o_hi, o_lo, projected, added = (sem(n) for n in ("o_full", "o_hi", "o_lo", "projected", "added"))

        block = ctx.enter_context(nc.Block())

        class Slot:

            def __init__(self, pair, parity, g, steady):
                self.pair, self.parity, self.g, self.steady = pair, parity, g, steady
                self.i = 2 * pair + parity
                self.s = 4 * self.i + g

            def has(self, lag):
                return self.steady or 0 <= self.s - lag < UNITS

            def batch_ok(self, ahead):
                return self.steady or 0 <= self.i + ahead < B

            def unit(self, lag):
                ahead, g = divmod(self.g - lag, G)
                return self.i + ahead, self.pair + (self.parity + ahead) // 2, (self.parity + ahead) % 2, g

            def batch(self, ahead):
                return self.i + ahead, self.pair + (self.parity + ahead) // 2, (self.parity + ahead) % 2

        def run(eng, body):
            for i in range(FIRST, LOOP_FROM):
                for g in range(G):
                    body(Slot(i // 2, i % 2, g, False))
            with eng.Fori(LOOP_FROM // 2, LOOP_TO // 2) as pair:
                for parity in range(2):
                    for g in range(G):
                        body(Slot(pair, parity, g, True))
            for i in range(LOOP_TO, LAST + 1):
                for g in range(G):
                    body(Slot(i // 2, i % 2, g, False))

        @block.sync
        def _(sp):
            sp.wait_ge(ready, 4)

            def settle(t):
                if t.steady:
                    sp.sem_inc(sp_passed, 1)

            def slot(t):
                i, s, g = t.i, t.s, t.g
                if g == 0 and t.batch_ok(3):
                    b, half, par = t.batch(3)
                    wait_from_first(sp, normed, 4 * (b - 2) + 4)
                    settle(t)
                    sp.dma_start(x_in[:, par, :, :], x_load[b]).then_inc(x_got[par], 16)
                if g == 0 and t.batch_ok(0):
                    b, half, par = t.batch(0)
                    wait_from_first(sp, valued, 4 * (b - 2) + 4)
                    settle(t)
                    sp.dma_start(v_sb[:, par, :], v_batch[b]).then_inc(v_got[par], 16)
                    wait_from_first(sp, scored, 4 * (b - 2) + 4)
                    settle(t)
                    for part, src in enumerate((k_hi_heads, k_hi_heads, k_lo_heads)):
                        sp.dma_start(k_stack[part * HD:(part + 1) * HD, par, :, :], src[b]).then_inc(k_got[par], 16)
                if g == 2 and t.batch_ok(1):
                    b, half, par = t.batch(1)
                    wait_from_first(sp, max_mm, 4 * (b - 2) + 4)
                    settle(t)
                    for j in range(J):
                        sp.dma_start(k_diag[j * HD:(j + 1) * HD, par, :, j * S:(j + 1) * S],
                                     k_hi_groups[b, j]).then_inc(diag_got[par], 16)
                if g % 2 == 0 and t.has(2):
                    b, half, par, h = t.unit(2)
                    sp.wait_ge(q_lo, s)
                    settle(t)
                    wait_from_first(sp, scored, s - 4)
                    for j in range(J):
                        rows = slice(j * HD, (j + 1) * HD)
                        for part, src in enumerate((0, 1, 0)):
                            sp.dma_start(q_stack[part * HD:(part + 1) * HD, h:h + 2, j, :],
                                         q_part[rows, h:h + 2, src, :]).then_inc(stacked[h // 2], 16)
                if t.has(2):
                    b, half, par, h = t.unit(2)
                    sp.wait_ge(max_rows, s - 1)
                    settle(t)
                    wait_from_first(sp, scored, s - 5)
                    for part in range(2):
                        sp.dma_start(q_stack[3 * HD + part:3 * HD + part + 1, h, :, :],
                                     max_row[part * J:(part + 1) * J, g % 2, :]).then_inc(max_stacked[h], 16)
                if t.has(4 * 3 + 1):
                    b, half, par, j = t.unit(4 * 3 + 1)
                    sp.wait_ge(added, s - 12)
                    settle(t)
                    sp.dma_start(out_tile[b, j], res[:, j, :]).then_inc(stored[j], 16)
                if t.has(4 * 3 - 2):
                    b, half, par, j = t.unit(4 * 3 - 2)
                    wait_from_first(sp, stored[j], 16 * b)
                    settle(t)
                    sp.dma_start(res[:, j, :], x_tile[b, j]).then_inc(res_got[j], 16)

            run(sp, slot)
            for j in range(TT):
                sp.wait_ge(stored[j], 16 * B)

        @block.tensor
        def _(pe):
            pe.wait_ge(ready, 4)

            def slot(t):
                i, s, g = t.i, t.s, t.g
                if t.has(3):
                    b, half, par, h = t.unit(3)
                    pe.wait_ge(stacked[h // 2], 16 * 3 * J * (b + 1))
                    pe.wait_ge(max_stacked[h], 16 * 2 * (b + 1))
                    if h == 0:
                        pe.wait_ge(k_got[par], 16 * 3 * (half + 1))
                    pe.wait_ge(max_red, s - 1 if t.steady else min(s - 1, UNITS))
                    if not t.steady:
                        wait_from_first(pe, exped, s - 3)
                    for j in range(J):
                        mm = nc.tensor.matmul(score_ps[0:S, j, :], k_stack[:, par, J * h + j, :], q_stack[:, h, j, :],
                                              start=True, stop=True)
                    mm.then_inc(scored, 1)
                if t.has(0):
                    if g == 0:
                        pe.wait_ge(h_lo, 4 * i + 4)
                    wait_from_first(pe, max_rows, s - 1)
                    if not t.steady:
                        wait_from_first(pe, h_lo, min(s + 4, UNITS))
                    for k in range(KT):
                        for w, h in ((0, 0), (0, 1), (1, 0)):
                            mm = nc.tensor.matmul(a_ps[:, :], wq[:, w, k, g * P:(g + 1) * P], h_t[:, t.parity, h, k, :],
                                                  start=(k == 0 and w == 0 and h == 0), stop=(k == KT - 1 and w == 1))
                    mm.then_inc(q_done, 1)
                if t.has(8):
                    if g == 0:
                        pe.wait_ge(recip_lo, i - 1)
                    wait_from_first(pe, added, s - 12)
                    for part in range(2):
                        mm = nc.tensor.matmul(b_ps[:, :], sel16[:, g * P:(g + 1) * P], recip_part[:, part, :],
                                              start=(part == 0), stop=(part == 1))
                    mm.then_inc(spread, 1)
                if t.has(3):
                    b, half, par, h = t.unit(3)
                    if h == 0:
                        pe.wait_ge(v_got[par], 16 * (half + 1))
                        wait_from_first(pe, recip_done, b)
                    pe.wait_ge(exped, s - 2)
                    wait_from_first(pe, o_copied, s - 3)
                    for j in range(J):
                        rows = slice(j * HD, (j + 1) * HD)
                        c = (J * h + j) * HD
                        nc.tensor.matmul(o_ps[rows, :], v_sb[:, par, c:c + HD], probs[:, (g + 1) % 2, j, :],
                                         start=True, stop=True)
                    for j in range(J):
                        rows = slice(j * HD, (j + 1) * HD)
                        mm = nc.tensor.matmul(sum_ps[rows, :], ones[:, h * HD:(h + 1) * HD], probs[:, (g + 1) % 2, j, :],
                                              start=(h == 0), stop=(h == G - 1))
                    mm.then_inc(valued, 1)
                if t.has(1):
                    b, half, par, h = t.unit(1)
                    pe.wait_ge(q_hi, s)
                    if h == 0:
                        pe.wait_ge(diag_got[par], 16 * J * (half + 1))
                    if not t.steady:
                        wait_from_first(pe, max_red, s - 1)
                    for q in range(TT):
                        mm = nc.tensor.matmul(score_ps[:, q, 0:J * S], q_part[:, h, 0, q * P:(q + 1) * P],
                                              k_diag[:, par, h, :], start=True, stop=True)
                    mm.then_inc(max_mm, 1)
                if t.batch_ok(1):
                    b, half, par = t.batch(1)
                    if g == 0:
                        pe.wait_ge(normed, 4 * b + 4)
                    if t.has(0):
                        pe.wait_ge(q_read, s + 1)
                    if not t.steady:
                        wait_from_first(pe, h_lo, s + 4)
                    for j in range(TT):
                        mm = nc.tensor.transpose(a_ps[:, j * P:(j + 1) * P], x_norm[:, par, j, g * P:(g + 1) * P], ident)
                    mm.then_inc(turned, 1)
                if t.has(12):
                    b, half, par = t.batch(-3)
                    if g == 0:
                        pe.wait_ge(o_lo, 4 * b + 4)
                    if t.has(8):
                        pe.wait_ge(o_full, s - 7)
                    else:
                        wait_from_first(pe, added, s - 12)
                    for k in range(KT):
                        for o, w in ((0, 0), (0, 1), (1, 0)):
                            mm = nc.tensor.matmul(b_ps[:, :], o_part[:, par, o, k, g * P:(g + 1) * P], wo[:, w, k, :],
                                                  start=(k == 0 and o == 0 and w == 0), stop=(k == KT - 1 and o == 1))
                    mm.then_inc(projected, 1)
                if t.has(1):
                    pe.wait_ge(max_lo, s)
                    if t.batch_ok(1):
                        pe.wait_ge(h_lo, s + 5)
                    elif t.has(0):
                        pe.wait_ge(q_read, s + 1)
                    if not t.steady:
                        wait_from_first(pe, max_rows, s - 1)
                    for q in range(TT):
                        mm = nc.tensor.transpose(max_ps[0:2 * J, q * P:(q + 1) * P], max_part[:, q, :], ident16[:, :])
                    mm.then_inc(max_t, 1)

            run(pe, slot)

        @block.scalar
        def _(act):
            act.wait_ge(ready, 4)

            def slot(t):
                i, s, g = t.i, t.s, t.g
                if t.has(2):
                    act.wait_ge(max_t, s - 1)
                    wait_from_first(act, max_stacked[g], 32 * i)
                    nc.scalar.activation(max_row[:, g % 2, :], max_ps[0:2 * J, 0:T], ACT.Copy).then_inc(max_rows, 1)
                if t.has(3):
                    act.wait_ge(scored, s - 2)
                    wait_from_first(act, valued, s - 4)
                    nc.scalar.activation(probs[:, (g + 1) % 2, :, :], score_ps[0:S, :, :], ACT.Exp,
                                         scale=exp_scale[0:S, :]).then_inc(exped, 1)
                if t.has(-9):
                    b, half, par, j = t.unit(-9)
                    if j == 0:
                        act.wait_ge(x_got[par], 16 * (half + 1))
                    wait_from_first(act, squared, s + 9)
                    wait_from_first(act, rstd_b, s + 6)
                    nc.scalar.activation(junk[:, :], x_in[:, par, j, :], ACT.Square,
                                         scale=D ** -0.5 / H_GAIN, accum_out=sumsq[:, j:j + 1]).then_inc(squared, 1)
                if t.has(-8):
                    b, half, par, j = t.unit(-8)
                    act.wait_ge(rstd_b, s + 9)
                    if j == 0:
                        wait_from_first(act, turned, 4 * (b - 2) + 4)
                    nc.scalar.activation(x_norm[:, par, j, :], x_in[:, par, j, :], ACT.Copy,
                                         scale=rstd[:, j:j + 1]).then_inc(normed, 1)
                if t.has(8):
                    b, half, par = t.batch(-2)
                    act.wait_ge(o_full, s - 7)
                    nc.scalar.activation(o_part[:, par, 0, g, :], o_norm[:, :], ACT.Copy).then_inc(o_hi, 1)
                if t.has(3):
                    b, half, par, h = t.unit(3)
                    act.wait_ge(valued, s - 2)
                    wait_from_first(act, o_full, s - 10)
                    nc.scalar.activation(o_raw[:, par, h, :], o_ps[:, :], ACT.Copy, scale=v_scale).then_inc(o_copied, 1)
                if t.has(0):
                    act.wait_ge(q_full, s + 1)
                    wait_from_first(act, stacked[g // 2], 16 * 3 * J * i)
                    nc.scalar.activation(q_part[:, g, 0, :], q_rot[:, :], ACT.Copy).then_inc(q_hi, 1)
                if t.batch_ok(1):
                    b, half, par = t.batch(1)
                    act.wait_ge(turned, s + 5)
                    nc.scalar.activation(h_t[:, par, 0, g, :], a_ps[:, :], ACT.Copy).then_inc(h_hi, 1)
                if g == G - 1 and t.batch_ok(-1):
                    act.wait_ge(recip_done, i)
                    wait_from_first(act, spread, 4 * (i - 2) + 4)
                    nc.scalar.activation(recip_part[:, 0, :], recip[:, :], ACT.Copy).then_inc(recip_hi, 1)

            run(act, slot)

        @block.gpsimd
        def _(pool):
            nc.gpsimd.memset(k_diag[:, :, :, :], 0.0).then_inc(zeroed, 1)
            pool.wait_ge(zeroed, 1)
            nc.gpsimd.memset(k_stack[3 * HD:STACK, :, :, :], -1.0).then_inc(ready, 1)
            pool.wait_ge(ready, 2)
            nc.gpsimd.memset(minus_half[:, :], -0.5).then_inc(ready, 1)
            nc.gpsimd.memset(scaled_eps[:, :], EPS / (H_GAIN * H_GAIN)).then_inc(ready, 1)
            pool.wait_ge(ready, 4)

            def slot(t):
                i, s, g = t.i, t.s, t.g
                if t.has(0):
                    pool.wait_ge(q_read, s + 1)
                    wait_from_first(pool, q_full, s)
                    nc.gpsimd.tensor_tensor(sin_part[:, :], swapped[:, :], sin_q, ALU.mult).then_inc(q_sin, 1)
                if t.has(8):
                    b, half, par = t.batch(-2)
                    pool.wait_ge(o_hi, s - 7)
                    nc.gpsimd.tensor_tensor(o_part[:, par, 1, g, :], o_norm[:, :], o_part[:, par, 0, g, :],
                                            ALU.subtract).then_inc(o_lo, 1)
                if t.has(0):
                    pool.wait_ge(q_hi, s + 1)
                    nc.gpsimd.tensor_tensor(q_part[:, g, 1, :], q_rot[:, :], q_part[:, g, 0, :],
                                            ALU.subtract).then_inc(q_lo, 1)
                if t.has(-9):
                    b, half, par, j = t.unit(-9)
                    pool.wait_ge(squared, s + 10)
                    nc.gpsimd.tensor_tensor(mean_eps[:, j:j + 1], sumsq[:, j:j + 1], scaled_eps[:, :],
                                            ALU.add).then_inc(rstd_a, 1)
                    pool.wait_ge(rstd_a, s + 10)
                    wait_from_first(pool, normed, s + 6)
                    nc.gpsimd.tensor_tensor(rstd[:, j:j + 1], mean_eps[:, j:j + 1], minus_half[:, :],
                                            ALU.pow).then_inc(rstd_b, 1)
                if g == G - 1 and t.batch_ok(-1):
                    pool.wait_ge(recip_hi, i)
                    nc.gpsimd.tensor_tensor(recip_part[:, 1, :], recip[:, :], recip_part[:, 0, :],
                                            ALU.subtract).then_inc(recip_lo, 1)

            run(pool, slot)

        @block.vector
        def _(dve):
            nc.vector.tensor_copy(ident16[:, :], ident).then_inc(ready, 1)
            dve.wait_ge(ready, 4)

            def slot(t):
                i, s, g = t.i, t.s, t.g
                if g == G - 1 and t.batch_ok(-1):
                    dve.wait_ge(valued, 4 * i)
                    wait_from_first(dve, recip_lo, i - 1)
                    nc.vector.reciprocal(recip[:, :], sum_ps[:, :]).then_inc(recip_done, 1)
                if t.has(0):
                    dve.wait_ge(q_done, s + 1)
                    wait_from_first(dve, q_sin, s)
                    wait_from_first(dve, q_full, s)
                    nc.vector.tensor_tensor(cos_part[:, :], a_ps[:, :], cos_q, ALU.mult)
                    nc.vector.stream_shuffle(swapped[:, :], a_ps[:, :], SWAP).then_inc(q_read, 1)
                if t.has(8):
                    b, half, par = t.batch(-2)
                    dve.wait_ge(spread, s - 7)
                    dve.wait_ge(o_copied, s - 7)
                    wait_from_first(dve, o_lo, s - 8)
                    nc.vector.tensor_tensor(o_norm[:, :], b_ps[:, :], o_raw[:, par, g, :], ALU.mult).then_inc(o_full, 1)
                if t.has(0):
                    dve.wait_ge(q_sin, s + 1)
                    dve.wait_ge(q_read, s + 1)
                    wait_from_first(dve, q_lo, s)
                    nc.vector.tensor_tensor(q_rot[:, :], cos_part[:, :], sin_part[:, :], ALU.add).then_inc(q_full, 1)
                if t.has(1):
                    dve.wait_ge(max_mm, s)
                    wait_from_first(dve, max_lo, s - 1)
                    nc.vector.tensor_reduce(maxima[:, :, :], score_ps[:, :, 0:J * S].rearrange("p q (j k) -> p q j k", k=S),
                                            AX.X, ALU.max).then_inc(max_red, 1)
                    dve.wait_ge(max_red, s)
                    wait_from_first(dve, max_t, s - 1)
                    nc.vector.tensor_copy(max_part[:, :, 0:J], maxima[:, :, :]).then_inc(max_hi, 1)
                    dve.wait_ge(max_hi, s)
                    nc.vector.tensor_tensor(max_part[:, :, J:2 * J], maxima[:, :, :], max_part[:, :, 0:J],
                                            ALU.subtract).then_inc(max_lo, 1)
                if t.batch_ok(1):
                    b, half, par = t.batch(1)
                    dve.wait_ge(h_hi, s + 5)
                    nc.vector.tensor_tensor(h_t[:, par, 1, g, :], a_ps[:, :], h_t[:, par, 0, g, :],
                                            ALU.subtract).then_inc(h_lo, 1)
                if t.has(12):
                    dve.wait_ge(projected, s - 11)
                    dve.wait_ge(res_got[g], 16 * (i - 2))
                    nc.vector.scalar_tensor_tensor(out=res[:, g, :], in0=b_ps[:, :], scalar=out_scale, in1=res[:, g, :],
                                                   op0=ALU.mult, op1=ALU.add).then_inc(added, 1)

            run(dve, slot)


def cross_attention(nc, x, ctx_in, norm_w, w_q, w_kv, w_o, consts_in, out):
    with ExitStack() as ctx:
        sb = lambda name, shape, dt: ctx.enter_context(nc.sbuf_tensor(name, shape, dt))
        k_hi_dram = nc.dram_tensor("k_hi_dram", [D, NTOK], F16, kind="Internal").ap()
        k_lo_dram = nc.dram_tensor("k_lo_dram", [D, NTOK], F16, kind="Internal").ap()
        v_dram = nc.dram_tensor("v_dram", [NTOK, D], F32, kind="Internal").ap()
        keep = (
            sb("consts", [P, C_END], F32),
            sb("wq", [P, 2, KT, D], F16),
            sb("wo", [P, 2, KT, D], F16),
            sb("sel16", [P, G * P], F16),
            sb("scales", [P, 4], F32),
        )
        setup_block(nc, keep, ctx_in.rearrange("b s d -> (b s) d"), norm_w, w_q, w_kv, w_o, consts_in,
                    k_hi_dram, k_lo_dram, v_dram)
        attention_block(nc, keep, x, out, k_hi_dram, k_lo_dram, v_dram)


def kernel(x, ctx_1024, L0_xattn_norm_w, L0_xattn_Wq, L0_xattn_Wkv, L0_xattn_Wo):
    import numpy as np
    import concourse.bacc as bacc
    from concourse.bass_utils import run_bass_kernel_spmd

    nc = bacc.Bacc("TRN2", target_bir_lowering=False, num_devices=1)
    arrays = {
        "x": np.ascontiguousarray(x), "ctx": np.ascontiguousarray(ctx_1024),
        "norm_w": np.ascontiguousarray(L0_xattn_norm_w), "w_q": np.ascontiguousarray(L0_xattn_Wq),
        "w_kv": np.ascontiguousarray(L0_xattn_Wkv), "w_o": np.ascontiguousarray(L0_xattn_Wo),
        "shape_constants": shape_constants(),
    }
    aps = [nc.dram_tensor(name, a.shape, mybir.dt.from_np(a.dtype), kind="ExternalInput").ap()
           for name, a in arrays.items()]
    out = nc.dram_tensor("out", (B, T, D), F32, kind="ExternalOutput").ap()
    cross_attention(nc, *aps, out)
    return run_bass_kernel_spmd(nc, [arrays], core_ids=[0]).results[0]["out"]
```

```python
from contextlib import ExitStack

import concourse.bass as bass
from concourse import mybir

F32 = mybir.dt.float32
F16 = mybir.dt.float16
ALU = mybir.AluOpType
ACT = mybir.ActivationFunctionType
AX = mybir.AxisListType
ABSMAX = bass.bass_isa.ReduceOp.absmax

P = 128
B, T, D = 32, 512, 512
S = 77
H, HD = 16, 32
KT = D // P
TT = T // P
G = H * HD // P
J = P // HD
UNITS = B * G
NTOK = B * S
CT = (NTOK + P - 1) // P
KCHUNK = (T // S) * S
EPS = 1e-6
TINY = 1e-30

W_TOP = 64.0
H_GAIN = 64.0
Q_GAIN = 1.0 / (W_TOP * H_GAIN)
K_TOP = 2.0
O_TOP = 256.0

STACK = 3 * HD + 2
SWAP = [(d + HD // 2) % HD for d in range(HD)]

C_ID, C_COSQ, C_SINQ = 0, P, P + T
C_COSK, C_SINK = P + 2 * T, P + 2 * T + S
C_END = P + 2 * T + 2 * S


def shape_constants():
    import numpy as np

    c = np.zeros((P, C_END), np.float32)
    c[:, C_ID:C_ID + P] = np.eye(P, dtype=np.float32)
    half = HD // 2
    freq = (np.float32(1.0) / np.float32(10000.0) ** (np.arange(half, dtype=np.float32) / np.float32(half)))
    feature = np.arange(P) % HD
    sign = np.where(feature < half, -1.0, 1.0).astype(np.float32)[:, None]
    column = np.arange(T)
    q_pos = (TT * (column % P) + column // P).astype(np.float32)
    q_ang = freq.astype(np.float32)[feature % half][:, None] * q_pos[None, :]
    k_ang = freq.astype(np.float32)[feature % half][:, None] * np.arange(S, dtype=np.float32)[None, :]
    c[:, C_COSQ:C_COSQ + T] = np.cos(q_ang) * np.float32(Q_GAIN)
    c[:, C_SINQ:C_SINQ + T] = np.sin(q_ang) * sign * np.float32(Q_GAIN)
    c[:, C_COSK:C_COSK + S] = np.cos(k_ang)
    c[:, C_SINK:C_SINK + S] = np.sin(k_ang) * sign
    return c


def wait_from_first(eng, sem, value):
    if not isinstance(value, int) or value > 0:
        eng.wait_ge(sem, value)


def setup_block(nc, sb_keep, x_ctx, norm_w, w_q, w_kv, w_o, consts_in, k_hi_dram, k_lo_dram, v_dram):
    consts, wq, wo, scales = sb_keep
    ident = consts[:, C_ID:C_ID + P]
    mats = [w_kv[0:D, :], w_kv[D:2 * D, :], w_q, w_o]
    W_ITEMS = len(mats) * KT
    ITEMS = W_ITEMS + CT
    chunks = [(c, min(KCHUNK, NTOK - c)) for c in range(0, NTOK, KCHUNK)]
    k_items = [(c, n, m) for c, n in chunks for m in range(G)]
    order = []
    for n in range(max(len(k_items), CT)):
        if n < len(k_items):
            order.append(("k", n))
        if n < CT:
            order.append(("v", n))
    CRING = 8

    def tokens(t):
        return min(P, NTOK - t * P)

    with ExitStack() as ctx:
        sb = lambda name, shape, dt=F32: ctx.enter_context(nc.sbuf_tensor(name, shape, dt))
        sem = lambda name: ctx.enter_context(nc.semaphore(name))
        w_nat = sb("w_nat", [P, 2, KT, D])
        w_t = sb("w_t", [P, len(mats), KT, D])
        w_col = sb("w_col", [P, KT])
        c_nat = sb("c_nat", [P, CRING, D])
        c_t = sb("c_t", [P, KT, NTOK])
        k_rot = sb("k_rot", [P, G, NTOK])
        k_hi = sb("k_hi", [P, NTOK], F16)
        k_lo = sb("k_lo", [P, NTOK], F16)
        v_row = sb("v_row", [P, 2, D])
        swapped = sb("k_swapped", [P, KCHUNK])
        cos_part = sb("k_cos_part", [P, KCHUNK])
        sin_part = sb("k_sin_part", [P, KCHUNK])
        peak = sb("peak", [P, len(k_items) + CT])
        tops = sb("tops", [P, 4])
        top_all = sb("top_all", [P, 4])
        inv = sb("inv", [P, 4])
        gain = sb("gain", [P, 4])
        tp = ctx.enter_context(nc.psum_tensor("tp", [P, 4, D], F32))
        kp = ctx.enter_context(nc.psum_tensor("kp", [P, 2, D], F32))
        vp = ctx.enter_context(nc.psum_tensor("vp", [P, 2, D], F32))

        const_in = sem("const_in")
        w_in = [sem(f"w_in{n}") for n in range(2)]
        c_in = [sem(f"c_in{n}") for n in range(CRING)]
        turned = sem("set_turned")
        copied_a = sem("copied_a")
        copied_v = sem("copied_v")
        k_done = sem("k_done")
        v_done = sem("v_done")
        k_read = sem("k_read")
        k_sin = sem("k_sin")
        k_full = sem("k_full")
        k_peak = sem("k_peak")
        v_copied = sem("v_copied")
        v_peaked = sem("v_peaked")
        v_out = [sem(f"v_out{n}") for n in range(2)]
        top_in = sem("top_in")
        top_out = sem("top_out")
        gained = sem("gained")
        step = sem("step")
        split_hi = sem("split_hi")
        split_lo = sem("split_lo")
        k_out = sem("k_out")

        block = ctx.enter_context(nc.Block())

        @block.sync
        def _(sp):
            sp.dma_start(consts[:, :], consts_in).then_inc(const_in, 16)
            sp.dma_start(w_col[:, :], norm_w.rearrange("(k p) -> p k", p=P), allow_slow_non_contiguous=True).then_inc(const_in, 16)
            for m, w in enumerate(mats):
                if m >= 2:
                    sp.wait_ge(turned, KT * (m - 1))
                sp.dma_start(w_nat[:, m % 2, :, :], w.rearrange("(t p) d -> p t d", p=P)).then_inc(w_in[m % 2], 16)
            for t in range(CT):
                n = tokens(t)
                if t >= CRING:
                    sp.wait_ge(turned, W_ITEMS + t - CRING + 1)
                sp.dma_start(c_nat[0:n, t % CRING, :], x_ctx[t * P:t * P + n, :]).then_inc(c_in[t % CRING], 16)
            for t in range(CT):
                n = tokens(t)
                sp.wait_ge(v_copied, t + 1)
                sp.dma_start(v_dram[t * P:t * P + n, :], v_row[0:n, t % 2, :]).then_inc(v_out[t % 2], 16)
            for m in range(G):
                rows = slice(m * P, (m + 1) * P)
                sp.wait_ge(split_hi, 3 + m)
                sp.dma_start(k_hi_dram[rows, :], k_hi[:, :]).then_inc(k_out, 16)
                sp.wait_ge(split_lo, 3 + m)
                sp.dma_start(k_lo_dram[rows, :], k_lo[:, :]).then_inc(k_out, 16)
            sp.wait_ge(k_out, 16 * 2 * G)
            for n in range(2):
                sp.wait_ge(v_out[n], 16 * ((CT + 1 - n) // 2))

        @block.tensor
        def _(pe):
            pe.wait_ge(const_in, 32)
            for item in range(ITEMS):
                if item >= 4:
                    pe.wait_ge(copied_v if item % 2 else copied_a, (item - 4) // 2 + 1)
                if item < W_ITEMS:
                    m, k = divmod(item, KT)
                    pe.wait_ge(w_in[m % 2], 16 * (m // 2 + 1))
                    for t in range(KT):
                        mm = nc.tensor.transpose(tp[:, item % 4, t * P:(t + 1) * P],
                                                 w_nat[:, m % 2, t, k * P:(k + 1) * P], ident)
                else:
                    t = item - W_ITEMS
                    n = tokens(t)
                    pe.wait_ge(c_in[t % CRING], 16 * (t // CRING + 1))
                    for k in range(KT):
                        mm = nc.tensor.transpose(tp[:, item % 4, k * P:k * P + n],
                                                 c_nat[0:n, t % CRING, k * P:(k + 1) * P], ident[0:n, 0:n])
                mm.then_inc(turned, 1)
            pe.wait_ge(copied_a, ITEMS // 2)
            pe.wait_ge(copied_v, ITEMS // 2)
            for kind, n in order:
                if kind == "k":
                    c, cols, m = k_items[n]
                    if n >= 2:
                        pe.wait_ge(k_read, n - 1)
                    for k in range(KT):
                        mm = nc.tensor.matmul(kp[:, n % 2, 0:cols], w_t[:, 0, k, m * P:(m + 1) * P],
                                              c_t[:, k, c:c + cols], start=(k == 0), stop=(k == KT - 1))
                    mm.then_inc(k_done, 1)
                else:
                    rows = tokens(n)
                    if n >= 2:
                        pe.wait_ge(v_copied, n - 1)
                        pe.wait_ge(v_peaked, n - 1)
                    for k in range(KT):
                        mm = nc.tensor.matmul(vp[0:rows, n % 2, :], c_t[:, k, n * P:n * P + rows],
                                              w_t[:, 1, k, :], start=(k == 0), stop=(k == KT - 1))
                    mm.then_inc(v_done, 1)

        def copy_item(eng, item):
            src = tp[:, item % 4, :]
            if item < W_ITEMS:
                m, k = divmod(item, KT)
                dst, scale = w_t[:, m, k, :], (w_col[:, k:k + 1] if m == 2 else None)
            else:
                t = item - W_ITEMS
                n = tokens(t)
                src = src.rearrange("p (k n) -> p k n", k=KT)[:, :, 0:n]
                dst, scale = c_t[:, :, t * P:t * P + n], None
            if eng == "act":
                return nc.scalar.activation(dst, src, ACT.Copy, scale=1.0 if scale is None else scale)
            if scale is None:
                return nc.vector.tensor_copy(dst, src)
            return nc.vector.tensor_scalar(dst, src, scale, None, ALU.mult)

        @block.scalar
        def _(act):
            act.wait_ge(const_in, 32)
            for item in range(0, ITEMS, 2):
                act.wait_ge(turned, item + 1)
                copy_item("act", item).then_inc(copied_a, 1)
            for n in range(CT):
                rows = tokens(n)
                act.wait_ge(v_done, n + 1)
                if n >= 2:
                    act.wait_ge(v_out[n % 2], 16 * (n // 2))
                act.wait_ge(v_peaked, n + 1)
                nc.scalar.activation(v_row[0:rows, n % 2, :], vp[0:rows, n % 2, :], ACT.Copy).then_inc(v_copied, 1)
            for m, w in enumerate((wq, wo)):
                act.wait_ge(gained, m + 1)
                nc.scalar.activation(w[:, 0, :, :], w_t[:, 2 + m, :, :], ACT.Copy,
                                     scale=gain[:, m:m + 1]).then_inc(split_hi, 1)
            act.wait_ge(gained, 3)
            for m in range(G):
                if m >= 1:
                    act.wait_ge(split_lo, 2 + m)
                    act.wait_ge(k_out, 32 * m)
                nc.scalar.activation(k_hi[:, :], k_rot[:, m, :], ACT.Copy, scale=gain[:, 2:3]).then_inc(split_hi, 1)

        @block.gpsimd
        def _(pool):
            for n, (c, cols, m) in enumerate(k_items):
                reps = cols // S
                pool.wait_ge(k_read, n + 1)
                if n >= 1:
                    pool.wait_ge(k_full, n)
                nc.gpsimd.tensor_tensor(
                    sin_part[:, 0:cols].rearrange("p (b s) -> p b s", s=S),
                    swapped[:, 0:cols].rearrange("p (b s) -> p b s", s=S),
                    consts[:, C_SINK:C_SINK + S].unsqueeze(1).to_broadcast([P, reps, S]), ALU.mult).then_inc(k_sin, 1)
            for n in range(4):
                pool.wait_ge(top_in, n + 1)
                nc.gpsimd.partition_all_reduce(top_all[:, n:n + 1], tops[:, n:n + 1], P, ABSMAX).then_inc(top_out, 1)

        @block.vector
        def _(dve):
            done = [0]

            def link(instruction):
                done[0] += 1
                instruction.then_inc(step, 1)
                dve.wait_ge(step, done[0])

            dve.wait_ge(const_in, 32)
            for item in range(1, ITEMS, 2):
                dve.wait_ge(turned, item + 1)
                copy_item("dve", item).then_inc(copied_v, 1)
            dve.wait_ge(copied_a, W_ITEMS // 2)
            dve.wait_ge(copied_v, W_ITEMS // 2)
            for m in range(2):
                nc.vector.tensor_reduce(tops[:, m:m + 1], w_t[:, 2 + m, :, :], AX.XY, ALU.max, apply_absolute_value=True).then_inc(top_in, 1)
            for kind, n in order:
                if kind == "k":
                    c, cols, m = k_items[n]
                    reps = cols // S
                    dve.wait_ge(k_done, n + 1)
                    if n >= 1:
                        dve.wait_ge(k_sin, n)
                        dve.wait_ge(k_full, n)
                    nc.vector.stream_shuffle(swapped[:, 0:cols], kp[:, n % 2, 0:cols], SWAP)
                    nc.vector.tensor_tensor(
                        cos_part[:, 0:cols].rearrange("p (b s) -> p b s", s=S),
                        kp[:, n % 2, 0:cols].rearrange("p (b s) -> p b s", s=S),
                        consts[:, C_COSK:C_COSK + S].unsqueeze(1).to_broadcast([P, reps, S]),
                        ALU.mult).then_inc(k_read, 1)
                    dve.wait_ge(k_read, n + 1)
                    dve.wait_ge(k_sin, n + 1)
                    nc.vector.tensor_tensor(k_rot[:, m, c:c + cols], cos_part[:, 0:cols], sin_part[:, 0:cols],
                                            ALU.add).then_inc(k_full, 1)
                    dve.wait_ge(k_full, n + 1)
                    nc.vector.tensor_reduce(peak[:, n:n + 1], k_rot[:, m, c:c + cols], AX.X,
                                            ALU.max, apply_absolute_value=True).then_inc(k_peak, 1)
                else:
                    rows = tokens(n)
                    if rows < P:
                        link(nc.vector.memset(peak[:, len(k_items) + n:len(k_items) + n + 1], 0.0))
                    dve.wait_ge(v_done, n + 1)
                    nc.vector.tensor_reduce(peak[0:rows, len(k_items) + n:len(k_items) + n + 1],
                                            vp[0:rows, n % 2, :], AX.X, ALU.max, apply_absolute_value=True).then_inc(v_peaked, 1)
            dve.wait_ge(k_peak, len(k_items))
            dve.wait_ge(v_peaked, CT)
            nc.vector.tensor_reduce(tops[:, 2:3], peak[:, 0:len(k_items)], AX.X, ALU.max).then_inc(top_in, 1)
            nc.vector.tensor_reduce(tops[:, 3:4], peak[:, len(k_items):len(k_items) + CT], AX.X, ALU.max).then_inc(top_in, 1)
            for n in range(4):
                dve.wait_ge(top_out, n + 1)
                link(nc.vector.tensor_scalar(top_all[:, n:n + 1], top_all[:, n:n + 1], TINY, None, ALU.max))
                link(nc.vector.reciprocal(inv[:, n:n + 1], top_all[:, n:n + 1]))
                nc.vector.tensor_scalar(gain[:, n:n + 1], inv[:, n:n + 1], (W_TOP, W_TOP, K_TOP, O_TOP)[n], None,
                                        ALU.mult).then_inc(gained, 1)
            dve.wait_ge(gained, 4)
            nc.vector.tensor_scalar(scales[:, 0:1], top_all[:, 0:1], top_all[:, 2:3], HD ** -0.5 / K_TOP, ALU.mult, ALU.mult)
            nc.vector.tensor_copy(scales[:, 1:2], gain[:, 3:4])
            nc.vector.tensor_scalar(scales[:, 2:3], top_all[:, 1:2], top_all[:, 3:4], 1.0 / (W_TOP * O_TOP), ALU.mult, ALU.mult)
            for m, w in enumerate((wq, wo)):
                dve.wait_ge(split_hi, m + 1)
                nc.vector.scalar_tensor_tensor(out=w[:, 1, :, :], in0=w_t[:, 2 + m, :, :], scalar=gain[:, m:m + 1],
                                               in1=w[:, 0, :, :], op0=ALU.mult, op1=ALU.subtract).then_inc(split_lo, 1)
            for m in range(G):
                dve.wait_ge(split_hi, 3 + m)
                if m >= 1:
                    dve.wait_ge(k_out, 32 * m)
                nc.vector.scalar_tensor_tensor(out=k_lo[:, :], in0=k_rot[:, m, :], scalar=gain[:, 2:3],
                                               in1=k_hi[:, :], op0=ALU.mult, op1=ALU.subtract).then_inc(split_lo, 1)


def attention_block(nc, sb_keep, x, out, k_hi_dram, k_lo_dram, v_dram):
    consts, wq, wo, scales = sb_keep
    ident = consts[:, C_ID:C_ID + P]
    cos_q = consts[:, C_COSQ:C_COSQ + T]
    sin_q = consts[:, C_SINQ:C_SINQ + T]
    exp_scale, v_gain, out_scale = scales[:, 0:1], scales[:, 1:2], scales[:, 2:3]

    x_load = x.rearrange("b (p j) d -> b p j d", j=TT)
    x_tile = x.rearrange("b (p j) d -> b j p d", j=TT)
    out_tile = out.rearrange("b (p j) d -> b j p d", j=TT)
    k_hi_heads = k_hi_dram.rearrange("(h d) (b s) -> b d h s", d=HD, s=S)
    k_lo_heads = k_lo_dram.rearrange("(h d) (b s) -> b d h s", d=HD, s=S)
    k_hi_groups = k_hi_dram.rearrange("(g j d) (b s) -> b j d g s", j=J, d=HD, s=S)
    v_batch = v_dram.rearrange("(b s) d -> b s d", s=S)

    FIRST, LAST = -3, B + 2
    READY = 5
    LO_V = 1
    LOOP_FROM, LOOP_TO = 4, B - 4

    with ExitStack() as ctx:
        sb = lambda name, shape, dt=F32: ctx.enter_context(nc.sbuf_tensor(name, shape, dt))
        ps = lambda name, shape: ctx.enter_context(nc.psum_tensor(name, shape, F32))
        sem = lambda name: ctx.enter_context(nc.semaphore(name))

        x_in = sb("x_in", [P, 2, TT, D])
        junk = sb("junk", [P, D], F16)
        sumsq = sb("sumsq", [P, TT])
        mean_eps = sb("mean_eps", [P, TT])
        scaled_eps = sb("scaled_eps", [P, 1])
        minus_half = sb("minus_half", [P, 1])
        rstd = sb("rstd", [P, TT])
        x_norm = sb("x_norm", [P, 2, TT, D])
        h_t = sb("h_t", [P, 2, 2, KT, T], F16)
        swapped = sb("swapped", [P, T])
        cos_part = sb("cos_part", [P, T])
        sin_part = sb("sin_part", [P, T])
        q_rot = sb("q_rot", [P, T])
        q_part = sb("q_part", [P, G, 2, T], F16)
        q_stack = sb("q_stack", [STACK, G, J, T], F16)
        k_stack = sb("k_stack", [STACK, 2, H, S], F16)
        k_diag = sb("k_diag", [P, 2, G, J * S], F16)
        v_sb = sb("v_sb", [S, 2, D])
        v_part = sb("v_part", [S, 2, H, 2 * HD + 1], F16)
        maxima = sb("maxima", [P, TT, J])
        max_part = sb("max_part", [P, TT, 2 * J], F16)
        max_row = sb("max_row", [2 * J, 2, T], F16)
        probs = sb("probs", [S, 2, J, T])
        p_part = sb("p_part", [S, 2, 2, J, T], F16)
        recip = sb("recip", [P, TT * J])
        o_norm = sb("o_norm", [P, TT, J * HD])
        o_part = sb("o_part", [P, 2, 2, G, T], F16)
        res = sb("res", [P, TT, D])

        score_ps = ps("score_ps", [P, J, T])
        o_ps = ps("o_ps", [P, 2, D])
        a_ps = ps("a_ps", [P, T])
        b_ps = ps("b_ps", [P, T])
        ident16 = sb("ident16", [P, P], F16)
        max_ps = a_ps[:, :].bitcast(F16)
        o_heads = o_ps[:, :, 0:TT * J // 2 * (HD + 1)].rearrange("p b (n c) -> p b n c", c=HD + 1)

        sp_passed = sem("sp_passed")
        zeroed = sem("zeroed")
        ready = sem("ready")
        x_got = [sem(f"x_got{n}") for n in range(2)]
        res_got = [sem(f"res_got{n}") for n in range(TT)]
        stored = [sem(f"stored{n}") for n in range(TT)]
        k_got = [sem(f"k_got{n}") for n in range(2)]
        diag_got = [sem(f"diag_got{n}") for n in range(2)]
        v_got = [sem(f"v_got{n}") for n in range(2)]
        stacked = [sem(f"stacked{n}") for n in range(2)]
        max_stacked = [sem(f"max_stacked{n}") for n in range(G)]
        squared, rstd_a, rstd_b, normed = sem("squared"), sem("rstd_a"), sem("rstd_b"), sem("normed")
        turned, h_hi, h_lo = sem("turned"), sem("h_hi"), sem("h_lo")
        q_done, q_read, q_sin, q_full, q_hi, q_lo = (sem(n) for n in ("q_done", "q_read", "q_sin", "q_full", "q_hi", "q_lo"))
        max_mm, max_red, max_hi, max_lo, max_t, max_rows = (
            sem(n) for n in ("max_mm", "max_red", "max_hi", "max_lo", "max_t", "max_rows"))
        scored, exped, p_hi, p_lo_v, p_lo_p, valued = (
            sem(n) for n in ("scored", "exped", "p_hi", "p_lo_v", "p_lo_p", "valued"))
        v_hi, v_lo = sem("v_hi"), sem("v_lo")
        recip_done, o_full, o_turned, o_hi, o_lo, projected, added = (
            sem(n) for n in ("recip_done", "o_full", "o_turned", "o_hi", "o_lo", "projected", "added"))

        block = ctx.enter_context(nc.Block())

        class Slot:

            def __init__(self, pair, parity, g, steady):
                self.pair, self.parity, self.g, self.steady = pair, parity, g, steady
                self.i = 2 * pair + parity
                self.s = 4 * self.i + g

            def has(self, lag):
                return self.steady or 0 <= self.s - lag < UNITS

            def batch_ok(self, ahead):
                return self.steady or 0 <= self.i + ahead < B

            def unit(self, lag):
                ahead, g = divmod(self.g - lag, G)
                return self.i + ahead, self.pair + (self.parity + ahead) // 2, (self.parity + ahead) % 2, g

            def batch(self, ahead):
                return self.i + ahead, self.pair + (self.parity + ahead) // 2, (self.parity + ahead) % 2

        def run(eng, body):
            for i in range(FIRST, LOOP_FROM):
                for g in range(G):
                    body(Slot(i // 2, i % 2, g, False))
            with eng.Fori(LOOP_FROM // 2, LOOP_TO // 2) as pair:
                for parity in range(2):
                    for g in range(G):
                        body(Slot(pair, parity, g, True))
            for i in range(LOOP_TO, LAST + 1):
                for g in range(G):
                    body(Slot(i // 2, i % 2, g, False))

        @block.sync
        def _(sp):
            sp.wait_ge(ready, READY)

            def settle(t):
                if t.steady:
                    sp.sem_inc(sp_passed, 1)

            def slot(t):
                i, s, g = t.i, t.s, t.g
                if t.has(2):
                    b, half, par, h = t.unit(2)
                    sp.wait_ge(max_rows, s - 1)
                    settle(t)
                    wait_from_first(sp, scored, s - 5)
                    for part in range(2):
                        sp.dma_start(q_stack[3 * HD + part:3 * HD + part + 1, h, :, :],
                                     max_row[part * J:(part + 1) * J, g % 2, :]).then_inc(max_stacked[h], 16)
                if t.has(11):
                    b, half, par, j = t.unit(11)
                    sp.wait_ge(added, s - 10)
                    settle(t)
                    sp.dma_start(out_tile[b, j], res[:, j, :]).then_inc(stored[j], 16)
                if t.has(8):
                    b, half, par, j = t.unit(8)
                    wait_from_first(sp, stored[j], 16 * b)
                    settle(t)
                    sp.dma_start(res[:, j, :], x_tile[b, j]).then_inc(res_got[j], 16)
                if g == 0 and t.batch_ok(3):
                    b, half, par = t.batch(3)
                    wait_from_first(sp, normed, 4 * (b - 2) + 4)
                    settle(t)
                    sp.dma_start(x_in[:, par, :, :], x_load[b]).then_inc(x_got[par], 16)
                if g == 0 and t.batch_ok(0):
                    b, half, par = t.batch(0)
                    wait_from_first(sp, v_lo, b - 1)
                    settle(t)
                    sp.dma_start(v_sb[:, par, :], v_batch[b]).then_inc(v_got[par], 16)
                    wait_from_first(sp, scored, 4 * (b - 2) + 4)
                    settle(t)
                    for part, src in enumerate((k_hi_heads, k_hi_heads, k_lo_heads)):
                        sp.dma_start(k_stack[part * HD:(part + 1) * HD, par, :, :], src[b]).then_inc(k_got[par], 16)
                if g == 2 and t.batch_ok(1):
                    b, half, par = t.batch(1)
                    wait_from_first(sp, max_mm, 4 * (b - 2) + 4)
                    settle(t)
                    for j in range(J):
                        sp.dma_start(k_diag[j * HD:(j + 1) * HD, par, :, j * S:(j + 1) * S],
                                     k_hi_groups[b, j]).then_inc(diag_got[par], 16)
                if g % 2 == 0 and t.has(2):
                    b, half, par, h = t.unit(2)
                    sp.wait_ge(q_lo, s)
                    settle(t)
                    wait_from_first(sp, scored, s - 4)
                    for j in range(J):
                        rows = slice(j * HD, (j + 1) * HD)
                        for part, src in enumerate((0, 1, 0)):
                            sp.dma_start(q_stack[part * HD:(part + 1) * HD, h:h + 2, j, :],
                                         q_part[rows, h:h + 2, src, :]).then_inc(stacked[h // 2], 16)

            run(sp, slot)
            for j in range(TT):
                sp.wait_ge(stored[j], 16 * B)

        @block.tensor
        def _(pe):
            pe.wait_ge(ready, READY)

            def slot(t):
                i, s, g = t.i, t.s, t.g
                if t.has(4):
                    b, half, par, h = t.unit(4)
                    pe.wait_ge(stacked[h // 2], 16 * 3 * J * (b + 1))
                    pe.wait_ge(max_stacked[h], 16 * 2 * (b + 1))
                    if h == 0:
                        pe.wait_ge(k_got[par], 16 * 3 * (half + 1))
                    pe.wait_ge(max_red, s - 1 if t.steady else min(s - 1, UNITS))
                    if not t.steady:
                        wait_from_first(pe, exped, s - 4)
                    for j in range(J):
                        mm = nc.tensor.matmul(score_ps[0:S, j, :], k_stack[:, par, J * h + j, :], q_stack[:, h, j, :],
                                              start=True, stop=True)
                    mm.then_inc(scored, 1)
                if t.has(0):
                    if g == 0:
                        pe.wait_ge(h_lo, 4 * i + 4)
                    wait_from_first(pe, max_rows, s - 1)
                    if not t.steady:
                        wait_from_first(pe, h_lo, min(s + 4, UNITS))
                    for k in range(KT):
                        for w, h in ((0, 0), (0, 1), (1, 0)):
                            mm = nc.tensor.matmul(a_ps[:, :], wq[:, w, k, g * P:(g + 1) * P], h_t[:, t.parity, h, k, :],
                                                  start=(k == 0 and w == 0 and h == 0), stop=(k == KT - 1 and w == 1))
                    mm.then_inc(q_done, 1)
                if t.has(6):
                    pe.wait_ge(o_full, s - 5)
                    wait_from_first(pe, added, s - 10)
                    for q in range(TT):
                        mm = nc.tensor.transpose(b_ps[:, q * P:(q + 1) * P], o_norm[:, q, :], ident)
                    mm.then_inc(o_turned, 1)
                if t.has(1):
                    b, half, par, h = t.unit(1)
                    pe.wait_ge(q_hi, s)
                    if h == 0:
                        pe.wait_ge(diag_got[par], 16 * J * (half + 1))
                    wait_from_first(pe, exped, s - 3)
                    if not t.steady:
                        wait_from_first(pe, max_red, s - 1)
                    for q in range(TT):
                        mm = nc.tensor.matmul(score_ps[:, q, 0:J * S], q_part[:, h, 0, q * P:(q + 1) * P],
                                              k_diag[:, par, h, :], start=True, stop=True)
                    mm.then_inc(max_mm, 1)
                if t.has(5):
                    b, half, par, h = t.unit(5)
                    u = (g + 1) % 2
                    if h == 0:
                        pe.wait_ge(v_lo, b + 1)
                    pe.wait_ge(p_lo_v, s - 4)
                    pe.wait_ge(p_lo_p, s - 4)
                    if not t.steady:
                        wait_from_first(pe, o_full, s - 5)
                    for q in range(TT):
                        for j in range(J):
                            head = J * h + j
                            cell = o_heads[:, q // 2, q % 2 * J + j, :]
                            hi, lo = (p_part[:, u, part, j, q * P:(q + 1) * P] for part in range(2))
                            nc.tensor.matmul(cell, hi, v_part[:, par, head, 0:HD + 1], start=True, stop=False)
                            nc.tensor.matmul(cell[:, 0:HD], hi, v_part[:, par, head, HD + 1:2 * HD + 1],
                                             start=False, stop=False)
                            mm = nc.tensor.matmul(cell, lo, v_part[:, par, head, 0:HD + 1], start=False, stop=True)
                    mm.then_inc(valued, 1)
                if t.batch_ok(1):
                    b, half, par = t.batch(1)
                    if g == 0:
                        pe.wait_ge(normed, 4 * b + 4)
                    if t.has(0):
                        pe.wait_ge(q_read, s + 1)
                    if not t.steady:
                        wait_from_first(pe, h_lo, s + 4)
                    for j in range(TT):
                        mm = nc.tensor.transpose(a_ps[:, j * P:(j + 1) * P], x_norm[:, par, j, g * P:(g + 1) * P], ident)
                    mm.then_inc(turned, 1)
                if t.has(10):
                    b, half, par, j = t.unit(10)
                    if j == 0:
                        pe.wait_ge(o_lo, 4 * b + 4)
                    if t.has(6):
                        pe.wait_ge(o_lo, s - 5)
                    else:
                        wait_from_first(pe, added, s - 10)
                    for k in range(KT):
                        for o, w in ((0, 0), (0, 1), (1, 0)):
                            mm = nc.tensor.matmul(b_ps[:, :], o_part[:, par, o, k, j * P:(j + 1) * P], wo[:, w, k, :],
                                                  start=(k == 0 and o == 0 and w == 0), stop=(k == KT - 1 and o == 1))
                    mm.then_inc(projected, 1)
                if t.has(1):
                    pe.wait_ge(max_lo, s)
                    if t.batch_ok(1):
                        pe.wait_ge(h_lo, s + 5)
                    elif t.has(0):
                        pe.wait_ge(q_read, s + 1)
                    if not t.steady:
                        wait_from_first(pe, max_rows, s - 1)
                    for q in range(TT):
                        mm = nc.tensor.transpose(max_ps[0:2 * J, q * P:(q + 1) * P], max_part[:, q, :], ident16[:, :])
                    mm.then_inc(max_t, 1)

            run(pe, slot)

        @block.scalar
        def _(act):
            act.wait_ge(ready, READY)

            def slot(t):
                i, s, g = t.i, t.s, t.g
                if t.has(2):
                    act.wait_ge(max_t, s - 1)
                    wait_from_first(act, max_stacked[g], 32 * i)
                    nc.scalar.activation(max_row[:, g % 2, :], max_ps[0:2 * J, 0:T], ACT.Copy).then_inc(max_rows, 1)
                if t.has(1):
                    b, half, par, h = t.unit(1)
                    act.wait_ge(q_full, s)
                    wait_from_first(act, stacked[h // 2], 16 * 3 * J * b)
                    nc.scalar.activation(q_part[:, h, 0, :], q_rot[:, :], ACT.Copy).then_inc(q_hi, 1)
                if t.has(4):
                    act.wait_ge(scored, s - 3)
                    wait_from_first(act, p_lo_v, s - 5)
                    wait_from_first(act, p_lo_p, s - 5)
                    nc.scalar.activation(probs[:, g % 2, :, :], score_ps[0:S, :, :], ACT.Exp,
                                         scale=exp_scale[0:S, :]).then_inc(exped, 1)
                if t.has(-9):
                    b, half, par, j = t.unit(-9)
                    if j == 0:
                        act.wait_ge(x_got[par], 16 * (half + 1))
                    wait_from_first(act, squared, s + 9)
                    wait_from_first(act, rstd_b, s + 6)
                    nc.scalar.activation(junk[:, :], x_in[:, par, j, :], ACT.Square,
                                         scale=D ** -0.5 / H_GAIN, accum_out=sumsq[:, j:j + 1]).then_inc(squared, 1)
                if t.has(6):
                    b, half, par, h = t.unit(6)
                    act.wait_ge(o_turned, s - 5)
                    wait_from_first(act, projected, 4 * (b - 2) + 4)
                    nc.scalar.activation(o_part[:, par, 0, h, :], b_ps[:, :], ACT.Copy).then_inc(o_hi, 1)
                if t.has(4):
                    act.wait_ge(exped, s - 3)
                    wait_from_first(act, valued, s - 5)
                    nc.scalar.activation(p_part[:, g % 2, 0, :, :], probs[:, g % 2, :, :], ACT.Copy).then_inc(p_hi, 1)
                if g == 2 and t.batch_ok(0):
                    b, half, par = t.batch(0)
                    act.wait_ge(v_got[par], 16 * (half + 1))
                    wait_from_first(act, valued, 4 * (b - 2) + 4)
                    nc.scalar.activation(v_part[:, par, :, 0:HD], v_sb[:, par, :].rearrange("s (h d) -> s h d", d=HD),
                                         ACT.Copy, scale=v_gain[0:S, :]).then_inc(v_hi, 1)
                if t.batch_ok(1):
                    b, half, par = t.batch(1)
                    act.wait_ge(turned, s + 5)
                    nc.scalar.activation(h_t[:, par, 0, g, :], a_ps[:, :], ACT.Copy).then_inc(h_hi, 1)
                if t.has(-8):
                    b, half, par, j = t.unit(-8)
                    act.wait_ge(rstd_b, s + 9)
                    if j == 0:
                        wait_from_first(act, turned, 4 * (b - 2) + 4)
                    nc.scalar.activation(x_norm[:, par, j, :], x_in[:, par, j, :], ACT.Copy,
                                         scale=rstd[:, j:j + 1]).then_inc(normed, 1)

            run(act, slot)

        @block.gpsimd
        def _(pool):
            nc.gpsimd.memset(k_diag[:, :, :, :], 0.0).then_inc(zeroed, 1)
            pool.wait_ge(zeroed, 1)
            nc.gpsimd.memset(k_stack[3 * HD:STACK, :, :, :], -1.0).then_inc(ready, 1)
            pool.wait_ge(ready, 2)
            nc.gpsimd.memset(minus_half[:, :], -0.5).then_inc(ready, 1)
            nc.gpsimd.memset(scaled_eps[:, :], EPS / (H_GAIN * H_GAIN)).then_inc(ready, 1)
            nc.gpsimd.memset(v_part[:, :, :, HD:HD + 1], 1.0).then_inc(ready, 1)
            pool.wait_ge(ready, READY)

            def slot(t):
                i, s, g = t.i, t.s, t.g
                if t.has(1):
                    b, half, par, h = t.unit(1)
                    pool.wait_ge(q_hi, s)
                    nc.gpsimd.tensor_tensor(q_part[:, h, 1, :], q_rot[:, :], q_part[:, h, 0, :],
                                            ALU.subtract).then_inc(q_lo, 1)
                if t.has(-9):
                    b, half, par, j = t.unit(-9)
                    pool.wait_ge(squared, s + 10)
                    nc.gpsimd.tensor_tensor(mean_eps[:, j:j + 1], sumsq[:, j:j + 1], scaled_eps[:, :],
                                            ALU.add).then_inc(rstd_a, 1)
                    pool.wait_ge(rstd_a, s + 10)
                    wait_from_first(pool, normed, s + 6)
                    nc.gpsimd.tensor_tensor(rstd[:, j:j + 1], mean_eps[:, j:j + 1], minus_half[:, :],
                                            ALU.pow).then_inc(rstd_b, 1)
                if t.has(0):
                    pool.wait_ge(q_read, s + 1)
                    wait_from_first(pool, q_full, s)
                    nc.gpsimd.tensor_tensor(sin_part[:, :], swapped[:, :], sin_q, ALU.mult).then_inc(q_sin, 1)
                if t.has(4):
                    pool.wait_ge(p_hi, s - 3)
                    nc.gpsimd.tensor_tensor(p_part[:, g % 2, 1, LO_V:J, :], probs[:, g % 2, LO_V:J, :],
                                            p_part[:, g % 2, 0, LO_V:J, :], ALU.subtract).then_inc(p_lo_p, 1)

            run(pool, slot)

        @block.vector
        def _(dve):
            nc.vector.tensor_copy(ident16[:, :], ident).then_inc(ready, 1)
            dve.wait_ge(ready, READY)

            def slot(t):
                i, s, g = t.i, t.s, t.g
                if t.has(1):
                    dve.wait_ge(q_sin, s)
                    dve.wait_ge(q_read, s)
                    wait_from_first(dve, q_lo, s - 1)
                    nc.vector.tensor_tensor(q_rot[:, :], cos_part[:, :], sin_part[:, :], ALU.add).then_inc(q_full, 1)
                if t.has(11):
                    b, half, par, j = t.unit(11)
                    dve.wait_ge(projected, s - 10)
                    dve.wait_ge(res_got[j], 16 * (b + 1))
                    nc.vector.scalar_tensor_tensor(out=res[:, j, :], in0=b_ps[:, :], scalar=out_scale, in1=res[:, j, :],
                                                   op0=ALU.mult, op1=ALU.add).then_inc(added, 1)
                if t.has(6):
                    dve.wait_ge(valued, s - 5)
                    wait_from_first(dve, o_full, s - 6)
                    nc.vector.reciprocal(recip[:, :].rearrange("p (b n) -> p b n", b=2),
                                         o_heads[:, :, :, HD]).then_inc(recip_done, 1)
                    dve.wait_ge(recip_done, s - 5)
                    wait_from_first(dve, o_turned, s - 6)
                    nc.vector.tensor_tensor(
                        o_norm[:, :, :].rearrange("p (b q) (j c) -> p b (q j) c", b=2, c=HD), o_heads[:, :, :, 0:HD],
                        recip[:, :].rearrange("p (b n) -> p b n", b=2).unsqueeze(3).to_broadcast([P, 2, TT * J // 2, HD]),
                        ALU.mult).then_inc(o_full, 1)
                if t.has(5):
                    u = (g + 1) % 2
                    dve.wait_ge(p_hi, s - 4)
                    nc.vector.tensor_tensor(p_part[:, u, 1, 0:LO_V, :], probs[:, u, 0:LO_V, :], p_part[:, u, 0, 0:LO_V, :],
                                            ALU.subtract).then_inc(p_lo_v, 1)
                if t.has(0):
                    dve.wait_ge(q_done, s + 1)
                    wait_from_first(dve, q_sin, s)
                    wait_from_first(dve, q_full, s)
                    nc.vector.tensor_tensor(cos_part[:, :], a_ps[:, :], cos_q, ALU.mult)
                    nc.vector.stream_shuffle(swapped[:, :], a_ps[:, :], SWAP).then_inc(q_read, 1)
                if t.has(6):
                    b, half, par, h = t.unit(6)
                    dve.wait_ge(o_hi, s - 5)
                    nc.vector.tensor_tensor(o_part[:, par, 1, h, :], b_ps[:, :], o_part[:, par, 0, h, :],
                                            ALU.subtract).then_inc(o_lo, 1)
                if t.has(1):
                    dve.wait_ge(max_mm, s)
                    wait_from_first(dve, max_lo, s - 1)
                    nc.vector.tensor_reduce(maxima[:, :, :], score_ps[:, :, 0:J * S].rearrange("p q (j k) -> p q j k", k=S),
                                            AX.X, ALU.max).then_inc(max_red, 1)
                    dve.wait_ge(max_red, s)
                    wait_from_first(dve, max_t, s - 1)
                    nc.vector.tensor_copy(max_part[:, :, 0:J], maxima[:, :, :]).then_inc(max_hi, 1)
                    dve.wait_ge(max_hi, s)
                    nc.vector.tensor_tensor(max_part[:, :, J:2 * J], maxima[:, :, :], max_part[:, :, 0:J],
                                            ALU.subtract).then_inc(max_lo, 1)
                if g == 2 and t.batch_ok(0):
                    b, half, par = t.batch(0)
                    dve.wait_ge(v_hi, b + 1)
                    nc.vector.scalar_tensor_tensor(
                        out=v_part[:, par, :, HD + 1:2 * HD + 1], in0=v_sb[:, par, :].rearrange("s (h d) -> s h d", d=HD),
                        scalar=v_gain[0:S, :], in1=v_part[:, par, :, 0:HD], op0=ALU.mult, op1=ALU.subtract).then_inc(v_lo, 1)
                if t.batch_ok(1):
                    b, half, par = t.batch(1)
                    dve.wait_ge(h_hi, s + 5)
                    nc.vector.tensor_tensor(h_t[:, par, 1, g, :], a_ps[:, :], h_t[:, par, 0, g, :],
                                            ALU.subtract).then_inc(h_lo, 1)

            run(dve, slot)


def cross_attention(nc, x, ctx_in, norm_w, w_q, w_kv, w_o, consts_in, out):
    with ExitStack() as ctx:
        sb = lambda name, shape, dt: ctx.enter_context(nc.sbuf_tensor(name, shape, dt))
        k_hi_dram = nc.dram_tensor("k_hi_dram", [D, NTOK], F16, kind="Internal").ap()
        k_lo_dram = nc.dram_tensor("k_lo_dram", [D, NTOK], F16, kind="Internal").ap()
        v_dram = nc.dram_tensor("v_dram", [NTOK, D], F32, kind="Internal").ap()
        keep = (
            sb("consts", [P, C_END], F32),
            sb("wq", [P, 2, KT, D], F16),
            sb("wo", [P, 2, KT, D], F16),
            sb("scales", [P, 4], F32),
        )
        setup_block(nc, keep, ctx_in.rearrange("b s d -> (b s) d"), norm_w, w_q, w_kv, w_o, consts_in,
                    k_hi_dram, k_lo_dram, v_dram)
        attention_block(nc, keep, x, out, k_hi_dram, k_lo_dram, v_dram)


def kernel(x, ctx_1024, L0_xattn_norm_w, L0_xattn_Wq, L0_xattn_Wkv, L0_xattn_Wo):
    import numpy as np
    import concourse.bacc as bacc
    from concourse.bass_utils import run_bass_kernel_spmd

    nc = bacc.Bacc("TRN2", target_bir_lowering=False, num_devices=1)
    arrays = {
        "x": np.ascontiguousarray(x), "ctx": np.ascontiguousarray(ctx_1024),
        "norm_w": np.ascontiguousarray(L0_xattn_norm_w), "w_q": np.ascontiguousarray(L0_xattn_Wq),
        "w_kv": np.ascontiguousarray(L0_xattn_Wkv), "w_o": np.ascontiguousarray(L0_xattn_Wo),
        "shape_constants": shape_constants(),
    }
    aps = [nc.dram_tensor(name, a.shape, mybir.dt.from_np(a.dtype), kind="ExternalInput").ap()
           for name, a in arrays.items()]
    out = nc.dram_tensor("out", (B, T, D), F32, kind="ExternalOutput").ap()
    cross_attention(nc, *aps, out)
    return run_bass_kernel_spmd(nc, [arrays], core_ids=[0]).results[0]["out"]
```

```python
from contextlib import ExitStack

import concourse.bass as bass
from concourse import mybir

F32 = mybir.dt.float32
F16 = mybir.dt.float16
ALU = mybir.AluOpType
ACT = mybir.ActivationFunctionType
AX = mybir.AxisListType
ABSMAX = bass.bass_isa.ReduceOp.absmax

P = 128
B, T, D = 32, 512, 512
S = 77
H, HD = 16, 32
KT = D // P
TT = T // P
G = H * HD // P
J = P // HD
UNITS = B * G
NTOK = B * S
CT = (NTOK + P - 1) // P
KCHUNK = (T // S) * S
EPS = 1e-6
NK = -(-NTOK // KCHUNK) * G
TINY = 1e-30

W_TOP = 64.0
H_GAIN = 64.0
Q_TOP = 0.125
Q_GAIN = Q_TOP / (W_TOP * H_GAIN)
K_TOP = 8.0
O_TOP = 256.0

STACK = 3 * HD + 2
FIRST, LAST = -3, B + 2
LOOP_FROM, LOOP_TO = 4, B - 4
LO_V = 1
SWAP = [(d + HD // 2) % HD for d in range(HD)]

C_ID, C_COSQ, C_SINQ = 0, P, P + T
C_COSK, C_SINK = P + 2 * T, P + 2 * T + S
C_END = P + 2 * T + 2 * S


def shape_constants():
    import numpy as np

    c = np.zeros((P, C_END), np.float32)
    c[:, C_ID:C_ID + P] = np.eye(P, dtype=np.float32)
    half = HD // 2
    freq = (np.float32(1.0) / np.float32(10000.0) ** (np.arange(half, dtype=np.float32) / np.float32(half)))
    feature = np.arange(P) % HD
    sign = np.where(feature < half, -1.0, 1.0).astype(np.float32)[:, None]
    column = np.arange(T)
    q_pos = (TT * (column % P) + column // P).astype(np.float32)
    q_ang = freq.astype(np.float32)[feature % half][:, None] * q_pos[None, :]
    k_ang = freq.astype(np.float32)[feature % half][:, None] * np.arange(S, dtype=np.float32)[None, :]
    c[:, C_COSQ:C_COSQ + T] = np.cos(q_ang) * np.float32(Q_GAIN)
    c[:, C_SINQ:C_SINQ + T] = np.sin(q_ang) * sign * np.float32(Q_GAIN)
    c[:, C_COSK:C_COSK + S] = np.cos(k_ang)
    c[:, C_SINK:C_SINK + S] = np.sin(k_ang) * sign
    return c


def wait_from_first(eng, sem, value):
    if not isinstance(value, int) or value > 0:
        eng.wait_ge(sem, value)


class Slot:

    def __init__(self, pair, parity, g, steady):
        self.pair, self.parity, self.g, self.steady = pair, parity, g, steady
        self.i = 2 * pair + parity
        self.s = 4 * self.i + g

    def has(self, lag):
        return self.steady or 0 <= self.s - lag < UNITS

    def batch_ok(self, ahead):
        return self.steady or 0 <= self.i + ahead < B

    def unit(self, lag):
        ahead, g = divmod(self.g - lag, G)
        return self.i + ahead, self.pair + (self.parity + ahead) // 2, (self.parity + ahead) % 2, g

    def batch(self, ahead):
        return self.i + ahead, self.pair + (self.parity + ahead) // 2, (self.parity + ahead) % 2


class Input:

    def __init__(self, nc, ctx, x, ident):
        sb = lambda name, shape, dt=F32: ctx.enter_context(nc.sbuf_tensor(name, shape, dt))
        sem = lambda name: ctx.enter_context(nc.semaphore(name))
        self.nc, self.ident = nc, ident
        self.x_load = x.rearrange("b (p j) d -> b p j d", j=TT)
        self.x_in = sb("x_in", [P, 2, TT, D])
        self.junk = sb("junk", [P, D], F16)
        self.sumsq = sb("sumsq", [P, TT])
        self.mean_eps = sb("mean_eps", [P, TT])
        self.scaled_eps = sb("scaled_eps", [P, 1])
        self.minus_half = sb("minus_half", [P, 1])
        self.rstd = sb("rstd", [P, TT])
        self.x_norm = sb("x_norm", [P, 2, TT, D])
        self.h_t = sb("h_t", [P, 2, 2, KT, T], F16)
        self.x_got = [sem(f"x_got{n}") for n in range(2)]
        self.squared = sem("squared")
        self.rstd_a = sem("rstd_a")
        self.rstd_b = sem("rstd_b")
        self.normed = sem("normed")
        self.turned = sem("turned")
        self.h_hi = sem("h_hi")
        self.h_lo = sem("h_lo")

    def square(self, act, t):
        b, half, par, j = t.unit(-9)
        if j == 0:
            act.wait_ge(self.x_got[par], 16 * (half + 1))
        wait_from_first(act, self.squared, t.s + 9)
        wait_from_first(act, self.rstd_b, t.s + 6)
        self.nc.scalar.activation(self.junk[:, :], self.x_in[:, par, j, :], ACT.Square, scale=D ** -0.5 / H_GAIN,
                                  accum_out=self.sumsq[:, j:j + 1]).then_inc(self.squared, 1)

    def root(self, pool, t):
        b, half, par, j = t.unit(-9)
        pool.wait_ge(self.squared, t.s + 10)
        self.nc.gpsimd.tensor_tensor(self.mean_eps[:, j:j + 1], self.sumsq[:, j:j + 1], self.scaled_eps[:, :],
                                     ALU.add).then_inc(self.rstd_a, 1)
        pool.wait_ge(self.rstd_a, t.s + 10)
        wait_from_first(pool, self.normed, t.s + 6)
        self.nc.gpsimd.tensor_tensor(self.rstd[:, j:j + 1], self.mean_eps[:, j:j + 1], self.minus_half[:, :],
                                     ALU.pow).then_inc(self.rstd_b, 1)

    def normalise(self, act, t):
        b, half, par, j = t.unit(-8)
        act.wait_ge(self.rstd_b, t.s + 9)
        if j == 0:
            wait_from_first(act, self.turned, 4 * (b - 2) + 4)
        self.nc.scalar.activation(self.x_norm[:, par, j, :], self.x_in[:, par, j, :], ACT.Copy,
                                  scale=self.rstd[:, j:j + 1]).then_inc(self.normed, 1)

    def turn(self, pe, t, bank):
        b, half, par = t.batch(1)
        for j in range(TT):
            mm = self.nc.tensor.transpose(bank[:, j * P:(j + 1) * P],
                                          self.x_norm[:, par, j, t.g * P:(t.g + 1) * P], self.ident)
        mm.then_inc(self.turned, 1)

    def high(self, act, t, bank):
        b, half, par = t.batch(1)
        act.wait_ge(self.turned, t.s + 5)
        self.nc.scalar.activation(self.h_t[:, par, 0, t.g, :], bank[:, :], ACT.Copy).then_inc(self.h_hi, 1)

    def low(self, dve, t, bank):
        b, half, par = t.batch(1)
        dve.wait_ge(self.h_hi, t.s + 5)
        self.nc.vector.tensor_tensor(self.h_t[:, par, 1, t.g, :], bank[:, :], self.h_t[:, par, 0, t.g, :],
                                     ALU.subtract).then_inc(self.h_lo, 1)


def setup_block(nc, sb_keep, stores, inp, x_ctx, norm_w, w_q, w_kv, w_o, consts_in, k_hi_dram, k_lo_dram, v_dram):
    consts, wq, wo, scales = sb_keep
    k_part, v_row, k_out, v_out = stores
    ident = consts[:, C_ID:C_ID + P]
    V, K, Q, O = range(4)
    mats = [w_kv[D:2 * D, :], w_kv[0:D, :], w_q, w_o]
    chunks = [(c, min(KCHUNK, NTOK - c)) for c in range(0, NTOK, KCHUNK)]
    k_items = [(q, m) for q in range(len(chunks)) for m in range(G)]
    fill = [Slot(i // 2, i % 2, g, False) for i in range(FIRST, 0) for g in range(G)]
    LATE = 9
    CRING, NRING = 5, 3
    BANKS, DIAGS = 3, 4

    def tokens(t):
        return min(P, NTOK - t * P)

    order = [("square", 0), ("norm", 0), ("gain", V), ("turn", "c", 0, 0), ("square", 1), ("norm", 1), ("turn", "c", 1, 0)]
    order += [("turn", "w", V, k) for k in range(KT)] + [("square", 2), ("norm", 2), ("square", 3), ("gain", K)]
    beside = {t: [("turn", "w", K, t)] for t in range(KT)}
    for n in range(2 * KT):
        beside.setdefault(1 + n, []).append(("w_square", *divmod(n, KT)))
    for q, (c, cols) in enumerate(chunks):
        beside.setdefault(min((c + cols + P - 1) // P, CT - 1), []).append(("table", q))
    for t in range(CT):
        if t + 4 < CT:
            order.append(("square", t + 4))
        if t + 3 < CT:
            order.append(("norm", t + 3))
        order += [("value", n) for n in range(CT - LATE) if (n + 1) * CT // (CT - LATE) - 1 == t]
        if t + 2 < CT:
            order.append(("turn", "c", t + 2, 0))
        order.append(("spread", t))
        order += beside.get(t, [])
    order.append(("scales",))
    late = {4: [("gain", Q)], 10: [("gain", O), ("undo",)]}
    for m, first in ((Q, 6), (O, 12)):
        for k in range(KT):
            late.setdefault(first + k, []).append(("turn", "w", m, k))
    for n in range(LATE):
        late.setdefault((n + 1) * NK // LATE - 1, []).append(("value", CT - LATE + n))
    for n in range(NK):
        order.append(("key", n))
        order += [("fill", fill[f]) for f in range(n * len(fill) // (NK - G), (n + 1) * len(fill) // (NK - G)) if f < len(fill)]
        order += late.get(n, [])
    turns = [step for step in order if step[0] == "turn"]
    number = {step: z for z, step in enumerate(turns)}

    with ExitStack() as ctx:
        sb = lambda name, shape, dt=F32: ctx.enter_context(nc.sbuf_tensor(name, shape, dt))
        sem = lambda name: ctx.enter_context(nc.semaphore(name))
        ps = lambda name, shape: ctx.enter_context(nc.psum_tensor(name, shape, F32))
        w_nat = sb("w_nat", [P, 2, KT, D])
        kv_t = sb("kv_t", [P, 2, 2, KT, D], F16)
        w_col = sb("w_col", [P, KT])
        q_col = sb("q_col", [P, KT])
        c_nat = sb("c_nat", [P, CRING, D])
        c_norm = sb("c_norm", [P, NRING, D])
        c_t = sb("c_t", [P, 2, KT, NTOK], F16)
        c_mean = sb("c_mean", [P, CT])
        c_floor = sb("c_floor", [P, CT])
        c_scale = sb("c_scale", [P, CT])
        c_size = sb("c_size", [P, CT])
        c_diag = sb("c_diag", [P, DIAGS, P])
        n_row = sb("n_row", [P, NTOK])
        n_sin = sb("n_sin", [P, NTOK])
        swapped = sb("k_swapped", [P, 2, KCHUNK])
        cos_part = sb("k_cos_part", [P, 2, KCHUNK])
        sin_part = sb("k_sin_part", [P, 2, KCHUNK])
        k_rot = sb("k_rot", [P, 2, KCHUNK])
        s_junk = sb("s_junk", [P, D], F16)
        w_square = sb("w_square", [P, 2 * KT])
        ones = sb("ones", [P, P])
        tiny = sb("tiny", [P, 1])
        halves = sb("halves", [P, 2])
        tops = sb("tops", [P, 8])
        top_all = sb("top_all", [P, 8])
        w_top = sb("w_top", [P, 4])
        inv = sb("inv", [P, 4])
        gain = sb("gain", [P, 4])
        bound2 = sb("bound2", [P, 2])
        root = sb("root", [P, 2])
        bound = sb("bound", [P, 2])
        bound_inv = sb("bound_inv", [P, 2])
        k_gain = sb("k_gain", [P, 1])
        product = sb("product", [P, 2])
        tp = ps("tp", [P, BANKS, D])
        hp = ps("hp", [P, T])
        kp = ps("kp", [P, 2, D])
        vp = ps("vp", [P, 2, D])

        ident_in, const_in, col_in = sem("ident_in"), sem("const_in"), sem("col_in")
        set_ready = sem("set_ready")
        w_in = [sem(f"w_in{n}") for n in range(2)]
        c_in = [sem(f"c_in{n}") for n in range(CRING)]
        c_squared = sem("c_squared")
        c_floored = sem("c_floored")
        c_rooted = sem("c_rooted")
        c_normed = sem("c_normed")
        c_sized = sem("c_sized")
        c_diagonal = sem("c_diagonal")
        n_spread = sem("n_spread")
        n_copied = sem("n_copied")
        w_squared = sem("w_squared")
        top_in = sem("top_in")
        top_out = sem("top_out")
        gained = sem("gained")
        turned = sem("set_turned")
        hi_done = sem("hi_done")
        lo_done = sem("lo_done")
        v_done = sem("v_done")
        v_copied = sem("v_copied")
        row_top_in, row_top_out = sem("row_top_in"), sem("row_top_out")
        bounded2 = sem("bounded2")
        rooted = sem("rooted")
        scaled = sem("scaled")
        step_done = sem("step_done")
        sined, tabled = sem("sined"), sem("tabled")
        k_done = sem("k_done")
        k_read = sem("k_read")
        k_sin = sem("k_sin")
        k_full = sem("k_full")
        k_hi = sem("k_hi")
        k_lo = sem("k_lo")

        block = ctx.enter_context(nc.Block())

        def size(n):
            return chunks[k_items[n][0]][1]

        def key_sum(eng, do, n):
            eng.wait_ge(k_read, n + 1)
            eng.wait_ge(k_sin, n + 1)
            if n >= 2:
                eng.wait_ge(k_lo, n - 1)
            if n >= 1:
                eng.wait_ge(k_full, n)
            do.tensor_tensor(k_rot[:, n % 2, 0:size(n)], cos_part[:, n % 2, 0:size(n)],
                             sin_part[:, n % 2, 0:size(n)], ALU.add).then_inc(k_full, 1)

        @block.sync
        def _(sp):
            def load_w(m):
                if m >= 2:
                    sp.wait_ge(turned, number["turn", "w", m - 2, KT - 1] + 1)
                    sp.wait_ge(w_squared, 2 * KT)
                    sp.wait_ge(gained, m - 1)
                sp.dma_start(w_nat[:, m % 2, :, :], mats[m].rearrange("(t p) d -> p t d", p=P)).then_inc(w_in[m % 2], 16)

            def load_c(t):
                n = tokens(t)
                if t >= CRING:
                    sp.wait_ge(c_normed, t - CRING + 1)
                sp.dma_start(c_nat[0:n, t % CRING, :], x_ctx[t * P:t * P + n, :]).then_inc(c_in[t % CRING], 16)

            load_c(0)
            sp.dma_start(consts[:, C_ID:C_ID + P], consts_in[:, C_ID:C_ID + P]).then_inc(ident_in, 16)
            load_w(V)
            for t in range(1, 4):
                load_c(t)
            load_w(K)
            sp.dma_start(w_col[:, :], norm_w.rearrange("(k p) -> p k", p=P), allow_slow_non_contiguous=True).then_inc(col_in, 16)
            for t in range(4, CT):
                load_c(t)
                if t == CRING:
                    sp.dma_start(consts[:, P:C_END], consts_in[:, P:C_END]).then_inc(const_in, 16)
            def load_x(b):
                sp.dma_start(inp.x_in[:, b, :, :], inp.x_load[b]).then_inc(inp.x_got[b], 16)

            load_x(0)

            def store_keys(n):
                q, m = k_items[n]
                c, cols = chunks[q]
                rows = slice(m * P, (m + 1) * P)
                sp.wait_ge(k_hi, n + 1)
                sp.dma_start(k_hi_dram[rows, c:c + cols], k_part[:, n % 2, 0, 0:cols]).then_inc(k_out[n % 2], 16)
                sp.wait_ge(k_lo, n + 1)
                sp.dma_start(k_lo_dram[rows, c:c + cols], k_part[:, n % 2, 1, 0:cols]).then_inc(k_out[n % 2], 16)

            for step in order:
                if step[0] == "key":
                    if step[1] >= 2:
                        store_keys(step[1] - 2)
                    if step[1] == 0:
                        load_w(Q)
                    elif step[1] == 3:
                        load_x(1)
                    elif step[1] == 5:
                        load_w(O)
                elif step[0] == "fill" and step[1].i == -1 and step[1].g == 0:
                    sp.wait_ge(inp.normed, TT)
                    sp.dma_start(inp.x_in[:, 0, :, :], inp.x_load[2]).then_inc(inp.x_got[0], 16)
            store_keys(NK - 2)
            store_keys(NK - 1)

        @block.tensor
        def _(pe):
            pe.wait_ge(ident_in, 16)
            pe.wait_ge(set_ready, 6)
            for step in order:
                if step[0] == "turn":
                    z = number[step]
                    if z >= BANKS:
                        pe.wait_ge(lo_done, z - BANKS + 1)
                    _, what, m, k = step
                    if what == "w":
                        pe.wait_ge(w_in[m % 2], 16 * (m // 2 + 1))
                        for t in range(KT):
                            mm = nc.tensor.transpose(tp[:, z % BANKS, t * P:(t + 1) * P],
                                                     w_nat[:, m % 2, t, k * P:(k + 1) * P], ident)
                    else:
                        t, n = m, tokens(m)
                        pe.wait_ge(c_normed, t + 1)
                        for k in range(KT):
                            mm = nc.tensor.transpose(tp[:, z % BANKS, k * P:k * P + n],
                                                     c_norm[0:n, t % NRING, k * P:(k + 1) * P], ident[0:n, 0:n])
                    mm.then_inc(turned, 1)
                elif step[0] == "spread":
                    t, n = step[1], tokens(step[1])
                    pe.wait_ge(c_diagonal, t + 1)
                    wait_from_first(pe, n_copied, t)
                    nc.tensor.matmul(hp[:, 0:n], ones[0:n, :], c_diag[0:n, t % DIAGS, 0:n],
                                     start=True, stop=True).then_inc(n_spread, 1)
                elif step[0] == "value":
                    t, rows = step[1], tokens(step[1])
                    last = max(number["turn", "c", t, 0], number["turn", "w", V, KT - 1])
                    pe.wait_ge(lo_done, last + 1)
                    if t >= 2:
                        pe.wait_ge(v_copied, t - 1)
                    for k in range(KT):
                        for h, w in ((0, 0), (0, 1), (1, 0)):
                            mm = nc.tensor.matmul(vp[0:rows, t % 2, :], c_t[:, h, k, t * P:t * P + rows],
                                                  kv_t[:, V, w, k, :], start=(k == 0 and h == 0 and w == 0),
                                                  stop=(k == KT - 1 and h == 1))
                    mm.then_inc(v_done, 1)
                elif step[0] == "key":
                    n = step[1]
                    q, m = k_items[n]
                    c, cols = chunks[q]
                    if n == 0:
                        pe.wait_ge(lo_done, number["turn", "c", CT - 1, 0] + 1)
                    if n >= 2:
                        pe.wait_ge(k_read, n - 1)
                    for k in range(KT):
                        for w, h in ((0, 0), (0, 1), (1, 0)):
                            mm = nc.tensor.matmul(kp[:, n % 2, 0:cols], kv_t[:, K, w, k, m * P:(m + 1) * P],
                                                  c_t[:, h, k, c:c + cols], start=(k == 0 and h == 0 and w == 0),
                                                  stop=(k == KT - 1 and w == 1))
                    mm.then_inc(k_done, 1)
                elif step[0] == "fill" and step[1].batch_ok(1):
                    t = step[1]
                    if t.g == 0:
                        pe.wait_ge(inp.normed, TT)
                        pe.wait_ge(n_copied, CT)
                    wait_from_first(pe, inp.h_lo, t.s + 4)
                    inp.turn(pe, t, hp)

        def item(step):
            z = number[step]
            _, what, m, k = step
            src = tp[:, z % BANKS, :]
            if what == "c":
                n = tokens(m)
                src = src.rearrange("p (k n) -> p k n", k=KT)[:, :, 0:n]
                return src, [c_t[:, part, :, m * P:m * P + n] for part in range(2)], None
            dst = [(kv_t[:, m, part, k, :] if m in (V, K) else (wq, wo)[m - Q][:, part, k, :]) for part in range(2)]
            return src, dst, (q_col[:, k:k + 1] if m == Q else gain[:, m:m + 1])

        def value_out(eng, t):
            rows = tokens(t)
            eng.wait_ge(v_done, t + 1)
            eng.wait_ge(c_sized, t + 1)
            if t >= 1:
                eng.wait_ge(v_copied, t)
            if t >= 2:
                eng.wait_ge(v_out[t % 2], 16 * (t // 2))
            dst, src, size = v_row[0:rows, t % 2, :], vp[0:rows, t % 2, :], c_size[0:rows, t:t + 1]
            if t < CT - LATE:
                nc.vector.tensor_scalar(dst, src, size, None, ALU.mult).then_inc(v_copied, 1)
            else:
                nc.scalar.activation(dst, src, ACT.Copy, scale=size).then_inc(v_copied, 1)

        @block.scalar
        def _(act):
            taken = []

            def square(sem, rows, src, dst, scale):
                if taken:
                    act.wait_ge(taken[-1], taken.count(taken[-1]))
                nc.scalar.activation(s_junk[0:rows, :], src, ACT.Square, scale=scale, accum_out=dst).then_inc(sem, 1)
                taken.append(sem)

            def key_high(n):
                act.wait_ge(scaled, 1)
                act.wait_ge(k_full, n + 1)
                if n >= 2:
                    act.wait_ge(k_out[n % 2], 32 * (n // 2))
                nc.scalar.activation(k_part[:, n % 2, 0, 0:size(n)], k_rot[:, n % 2, 0:size(n)], ACT.Copy,
                                     scale=k_gain[:, :]).then_inc(k_hi, 1)

            def store_value(t):
                act.wait_ge(v_copied, t + 1)
                act.dma_start(v_dram[t * P:t * P + tokens(t), :], v_row[0:tokens(t), t % 2, :]).then_inc(v_out[t % 2], 16)

            act.wait_ge(set_ready, 6)
            for step in order:
                if step[0] == "square":
                    t, n = step[1], tokens(step[1])
                    act.wait_ge(c_in[t % CRING], 16 * (t // CRING + 1))
                    square(c_squared, n, c_nat[0:n, t % CRING, :], c_mean[0:n, t:t + 1], D ** -0.5 / H_GAIN)
                elif step[0] == "turn":
                    src, dst, scale = item(step)
                    act.wait_ge(turned, number[step] + 1)
                    if step[1] == "w":
                        act.wait_ge(gained, step[2] + 1)
                    nc.scalar.activation(dst[0], src, ACT.Copy, scale=1.0 if scale is None else scale).then_inc(hi_done, 1)
                elif step[0] == "w_square":
                    _, m, t = step
                    act.wait_ge(w_in[m % 2], 16)
                    square(w_squared, P, w_nat[:, m, t, :], w_square[:, m * KT + t:m * KT + t + 1], D ** -0.5)
                elif step[0] == "spread":
                    t, n = step[1], tokens(step[1])
                    act.wait_ge(n_spread, t + 1)
                    nc.scalar.activation(n_row[:, t * P:t * P + n], hp[:, 0:n], ACT.Copy).then_inc(n_copied, 1)
                elif step[0] == "value":
                    t = step[1]
                    if t >= CT - LATE:
                        value_out(act, t)
                        store_value(t)
                    elif t >= 1:
                        store_value(t - 1)
                    if t == CT - LATE - 1:
                        store_value(t)
                elif step[0] == "key" and step[1] >= 1:
                    key_high(step[1] - 1)
                elif step[0] == "fill":
                    t = step[1]
                    if t.has(-9):
                        inp.square(act, t)
                    if t.batch_ok(1):
                        inp.high(act, t, hp)
                    if t.has(-8):
                        inp.normalise(act, t)
            key_high(NK - 1)

        @block.gpsimd
        def _(pool):
            nc.gpsimd.memset(tiny[:, :], TINY).then_inc(set_ready, 1)
            nc.gpsimd.memset(inp.minus_half[:, :], -0.5).then_inc(set_ready, 1)
            nc.gpsimd.memset(inp.scaled_eps[:, :], EPS / (H_GAIN * H_GAIN)).then_inc(set_ready, 1)
            nc.gpsimd.memset(halves[:, :], 0.5).then_inc(set_ready, 1)
            nc.gpsimd.memset(c_floor[:, CT - 1:CT], 0.0).then_inc(set_ready, 1)
            pool.wait_ge(set_ready, 6)
            reduced = 0
            for step in order:
                if step[0] == "square":
                    t, n = step[1], tokens(step[1])
                    pool.wait_ge(c_squared, t + 1)
                    nc.gpsimd.tensor_tensor(c_floor[0:n, t:t + 1], c_mean[0:n, t:t + 1], tiny[0:n, :],
                                            ALU.add).then_inc(c_floored, 1)
                    pool.wait_ge(c_floored, t + 1)
                    nc.gpsimd.tensor_tensor(c_scale[0:n, t:t + 1], c_floor[0:n, t:t + 1], inp.minus_half[0:n, :],
                                            ALU.pow).then_inc(c_rooted, 1)
                elif step[0] == "gain":
                    m = step[1]
                    pool.wait_ge(top_in, m + 1 + (m >= Q))
                    if m == Q:
                        nc.gpsimd.partition_all_reduce(top_all[:, 4:5], tops[:, 4:5], P, ABSMAX).then_inc(top_out, 1)
                    nc.gpsimd.partition_all_reduce(top_all[:, m:m + 1], tops[:, m:m + 1], P, ABSMAX).then_inc(top_out, 1)
                elif step[0] == "scales":
                    pool.wait_ge(row_top_in, 3)
                    nc.gpsimd.partition_all_reduce(top_all[:, 5:8], tops[:, 5:8], P, ABSMAX).then_inc(row_top_out, 1)
                    pool.wait_ge(bounded2, 1)
                    nc.gpsimd.tensor_tensor(root[:, :], bound2[:, :], halves[:, :], ALU.pow).then_inc(rooted, 1)
                elif step[0] == "key":
                    n = step[1]
                    q, m = k_items[n]
                    c, cols = chunks[q]
                    pool.wait_ge(tabled, q + 1)
                    pool.wait_ge(k_read, n + 1)
                    if n >= 2:
                        pool.wait_ge(k_full, n - 1)
                    nc.gpsimd.tensor_tensor(sin_part[:, n % 2, 0:size(n)], swapped[:, n % 2, 0:size(n)],
                                            n_sin[:, c:c + cols], ALU.mult).then_inc(k_sin, 1)
                    if n % 3 < 2:
                        key_sum(pool, nc.gpsimd, n)
                elif step[0] == "fill" and step[1].has(-9):
                    inp.root(pool, step[1])

        @block.vector
        def _(dve):
            done = [0]

            def link(instruction):
                done[0] += 1
                instruction.then_inc(step_done, 1)
                dve.wait_ge(step_done, done[0])

            def key_low(n):
                dve.wait_ge(k_hi, n + 1)
                nc.vector.scalar_tensor_tensor(out=k_part[:, n % 2, 1, 0:size(n)], in0=k_rot[:, n % 2, 0:size(n)],
                                               scalar=k_gain[:, :], in1=k_part[:, n % 2, 0, 0:size(n)],
                                               op0=ALU.mult, op1=ALU.subtract).then_inc(k_lo, 1)

            nc.vector.memset(ones[:, :], 1.0).then_inc(set_ready, 1)
            dve.wait_ge(ident_in, 16)
            for step in order:
                if step[0] == "turn":
                    src, dst, scale = item(step)
                    dve.wait_ge(hi_done, number[step] + 1)
                    if scale is None:
                        nc.vector.tensor_tensor(dst[1], src, dst[0], ALU.subtract).then_inc(lo_done, 1)
                    else:
                        nc.vector.scalar_tensor_tensor(out=dst[1], in0=src, scalar=scale, in1=dst[0],
                                                       op0=ALU.mult, op1=ALU.subtract).then_inc(lo_done, 1)
                elif step[0] == "gain":
                    m = step[1]
                    if m == Q:
                        dve.wait_ge(col_in, 16)
                        nc.vector.tensor_reduce(tops[:, 4:5], w_col[:, :], AX.X, ALU.max,
                                                apply_absolute_value=True).then_inc(top_in, 1)
                    dve.wait_ge(w_in[m % 2], 16 * (m // 2 + 1))
                    nc.vector.tensor_reduce(tops[:, m:m + 1], w_nat[:, m % 2, :, :], AX.XY, ALU.max,
                                            apply_absolute_value=True).then_inc(top_in, 1)
                    dve.wait_ge(top_out, m + 1 + (m >= Q))
                    link(nc.vector.tensor_scalar(w_top[:, m:m + 1], top_all[:, m:m + 1],
                                                 top_all[:, 4:5] if m == Q else 1.0, TINY, ALU.mult, ALU.max))
                    link(nc.vector.reciprocal(inv[:, m:m + 1], w_top[:, m:m + 1]))
                    last = nc.vector.tensor_scalar(gain[:, m:m + 1], inv[:, m:m + 1], W_TOP, None, ALU.mult)
                    if m == Q:
                        link(last)
                        last = nc.vector.tensor_scalar(q_col[:, :], w_col[:, :], gain[:, m:m + 1], None, ALU.mult)
                    last.then_inc(gained, 1)
                elif step[0] == "norm":
                    t, n = step[1], tokens(step[1])
                    dve.wait_ge(c_rooted, t + 1)
                    if t >= NRING:
                        dve.wait_ge(turned, number["turn", "c", t - NRING, 0] + 1)
                    nc.vector.tensor_scalar(c_norm[0:n, t % NRING, :], c_nat[0:n, t % CRING, :], c_scale[0:n, t:t + 1], None,
                                            ALU.mult).then_inc(c_normed, 1)
                    nc.vector.reciprocal(c_size[0:n, t:t + 1], c_scale[0:n, t:t + 1]).then_inc(c_sized, 1)
                    dve.wait_ge(c_sized, t + 1)
                    if t >= DIAGS:
                        dve.wait_ge(n_spread, t - DIAGS + 1)
                    nc.vector.tensor_scalar(c_diag[0:n, t % DIAGS, :], ident[0:n, :], c_size[0:n, t:t + 1], None,
                                            ALU.mult).then_inc(c_diagonal, 1)
                elif step[0] == "value" and step[1] < CT - LATE:
                    value_out(dve, step[1])
                elif step[0] == "table":
                    q = step[1]
                    c, cols = chunks[q]
                    dve.wait_ge(const_in, 16)
                    dve.wait_ge(n_copied, (c + cols + P - 1) // P)
                    n_chunk, sin_chunk = (a[:, c:c + cols].rearrange("p (b s) -> p b s", s=S) for a in (n_row, n_sin))
                    cos_k, sin_k = (consts[:, col:col + S].unsqueeze(1).to_broadcast([P, cols // S, S])
                                    for col in (C_COSK, C_SINK))
                    nc.vector.tensor_tensor(sin_chunk, n_chunk, sin_k, ALU.mult).then_inc(sined, 1)
                    dve.wait_ge(sined, q + 1)
                    nc.vector.tensor_tensor(n_chunk, n_chunk, cos_k, ALU.mult).then_inc(tabled, 1)
                elif step[0] == "scales":
                    dve.wait_ge(w_squared, 2 * KT)
                    for m in (V, K):
                        nc.vector.tensor_reduce(tops[:, 5 + m:6 + m], w_square[:, m * KT:(m + 1) * KT],
                                                AX.X, ALU.max).then_inc(row_top_in, 1)
                    dve.wait_ge(c_floored, CT)
                    nc.vector.tensor_reduce(tops[:, 7:8], c_floor[:, :], AX.X, ALU.max).then_inc(row_top_in, 1)
                    dve.wait_ge(row_top_out, 1)
                    nc.vector.tensor_scalar(bound2[:, :], top_all[:, 5:7], top_all[:, 7:8], TINY,
                                            ALU.mult, ALU.max).then_inc(bounded2, 1)
                    dve.wait_ge(rooted, 1)
                    link(nc.vector.scalar_tensor_tensor(out=bound[:, :], in0=root[:, :], scalar=D * H_GAIN, in1=gain[:, 0:2],
                                                        op0=ALU.mult, op1=ALU.mult))
                    link(nc.vector.reciprocal(bound_inv[:, :], bound[:, :]))
                    nc.vector.tensor_scalar(scales[:, 1:2], bound_inv[:, V:V + 1], O_TOP, None, ALU.mult)
                    nc.vector.tensor_scalar(k_gain[:, :], bound_inv[:, K:K + 1], K_TOP, None, ALU.mult).then_inc(scaled, 1)
                elif step[0] == "undo":
                    nc.vector.tensor_scalar(product[:, 0:1], w_top[:, Q:Q + 1], w_top[:, K:K + 1],
                                            HD ** -0.5 / (Q_TOP * K_TOP * W_TOP), ALU.mult, ALU.mult)
                    link(nc.vector.tensor_scalar(product[:, 1:2], w_top[:, O:O + 1], w_top[:, V:V + 1],
                                                 1.0 / (W_TOP * W_TOP * O_TOP), ALU.mult, ALU.mult))
                    nc.vector.tensor_tensor(scales[:, 0:1], product[:, 0:1], bound[:, K:K + 1], ALU.mult)
                    nc.vector.tensor_tensor(scales[:, 2:3], product[:, 1:2], bound[:, V:V + 1], ALU.mult)
                elif step[0] == "key":
                    n = step[1]
                    q, m = k_items[n]
                    c, cols = chunks[q]
                    dve.wait_ge(tabled, q + 1)
                    dve.wait_ge(k_done, n + 1)
                    if n >= 2:
                        dve.wait_ge(k_sin, n - 1)
                        dve.wait_ge(k_full, n - 1)
                    nc.vector.tensor_tensor(cos_part[:, n % 2, 0:size(n)], kp[:, n % 2, 0:size(n)],
                                            n_row[:, c:c + cols], ALU.mult)
                    nc.vector.stream_shuffle(swapped[:, n % 2, 0:size(n)], kp[:, n % 2, 0:size(n)], SWAP).then_inc(k_read, 1)
                    if n >= 1:
                        if n % 3 == 0:
                            key_sum(dve, nc.vector, n - 1)
                        key_low(n - 1)
                elif step[0] == "fill" and step[1].batch_ok(1):
                    inp.low(dve, step[1], hp)
            if NK % 3 == 0:
                key_sum(dve, nc.vector, NK - 1)
            key_low(NK - 1)


def attention_block(nc, sb_keep, stores, inp, x, out, k_hi_dram, k_lo_dram, v_dram):
    consts, wq, wo, scales = sb_keep
    _, _, k_out, v_out = stores
    ident = consts[:, C_ID:C_ID + P]
    cos_q = consts[:, C_COSQ:C_COSQ + T]
    sin_q = consts[:, C_SINQ:C_SINQ + T]
    exp_scale, v_gain, out_scale = scales[:, 0:1], scales[:, 1:2], scales[:, 2:3]

    out_pair = out.rearrange("b (p a j) d -> b a p j d", a=2, j=TT // 2)
    k_hi_heads = k_hi_dram.rearrange("(h d) (b s) -> b d h s", d=HD, s=S)
    k_lo_heads = k_lo_dram.rearrange("(h d) (b s) -> b d h s", d=HD, s=S)
    k_hi_groups = k_hi_dram.rearrange("(g j d) (b s) -> b j d g s", j=J, d=HD, s=S)
    v_batch = v_dram.rearrange("(b s) d -> b s d", s=S)

    READY = 3

    with ExitStack() as ctx:
        sb = lambda name, shape, dt=F32: ctx.enter_context(nc.sbuf_tensor(name, shape, dt))
        ps = lambda name, shape: ctx.enter_context(nc.psum_tensor(name, shape, F32))
        sem = lambda name: ctx.enter_context(nc.semaphore(name))

        h_t, h_lo = inp.h_t, inp.h_lo
        swapped = sb("swapped", [P, T])
        cos_part = sb("cos_part", [P, T])
        sin_part = sb("sin_part", [P, T])
        q_rot = sb("q_rot", [P, T])
        q_part = sb("q_part", [P, G, 2, T], F16)
        q_stack = sb("q_stack", [STACK, G, J, T], F16)
        k_stack = sb("k_stack", [STACK, 2, H, S], F16)
        k_diag = sb("k_diag", [P, 2, G, J * S], F16)
        v_sb = sb("v_sb", [S, 2, D])
        v_part = sb("v_part", [S, 2, H, 2 * HD + 1], F16)
        maxima = sb("maxima", [P, J, TT])
        max_part = sb("max_part", [P, 2, J, TT], F16)
        max_row = sb("max_row", [2 * J * TT, 2, P], F16)
        probs = sb("probs", [S, 2, J, T])
        p_part = sb("p_part", [S, 2, 2, J, T], F16)
        recip = sb("recip", [P, TT * J])
        o_norm = sb("o_norm", [P, TT, J * HD])
        o_part = sb("o_part", [P, 2, 2, G, T], F16)
        res = sb("res", [P, 2, TT, D])

        score_ps = ps("score_ps", [P, J, T])
        o_ps = ps("o_ps", [P, 2, D])
        a_ps = ps("a_ps", [P, T])
        b_ps = ps("b_ps", [P, T])
        ident16 = sb("ident16", [P, P], F16)
        SPARE = 4
        PROJECT = 9

        def turn_bank(t):
            return o_ps[:, 0, :] if not t.steady and t.s < SPARE else a_ps[:, :]

        def projection_bank(t, lag):
            if t.steady or t.s - lag <= UNITS:
                return b_ps
            return a_ps if t.s - lag < UNITS + 6 or (t.s - lag) % 2 else b_ps

        def max_bank(t, lag):
            if t.steady or t.s - lag >= PROJECT:
                return a_ps[:, :].bitcast(F16)
            return (o_ps[:, 1, :] if t.s - lag < SPARE else b_ps[:, :]).bitcast(F16)

        o_heads = o_ps[:, :, 0:TT * J // 2 * (HD + 1)].rearrange("p b (n c) -> p b n c", c=HD + 1)

        sp_passed = sem("sp_passed")
        zeroed = sem("zeroed")
        ready = sem("ready")
        res_got = [sem(f"res_got{n}") for n in range(2)]
        stored = [sem(f"stored{n}") for n in range(2)]
        k_got = [sem(f"k_got{n}") for n in range(2)]
        diag_got = [sem(f"diag_got{n}") for n in range(2)]
        v_got = [sem(f"v_got{n}") for n in range(2)]
        stacked = [sem(f"stacked{n}") for n in range(2)]
        first_stacked = sem("first_stacked")
        max_stacked = [sem(f"max_stacked{n}") for n in range(G)]
        q_done, q_read, q_sin, q_full, q_hi, q_lo = (sem(n) for n in ("q_done", "q_read", "q_sin", "q_full", "q_hi", "q_lo"))
        max_mm, max_red, max_hi, max_lo, max_t, max_rows = (
            sem(n) for n in ("max_mm", "max_red", "max_hi", "max_lo", "max_t", "max_rows"))
        scored, exped, p_hi, p_lo_v, p_lo_p, valued = (
            sem(n) for n in ("scored", "exped", "p_hi", "p_lo_v", "p_lo_p", "valued"))
        v_hi, v_lo = sem("v_hi"), sem("v_lo")
        recip_done, o_full, o_turned, o_hi, o_lo, projected, added = (
            sem(n) for n in ("recip_done", "o_full", "o_turned", "o_hi", "o_lo", "projected", "added"))

        block = ctx.enter_context(nc.Block())

        def run(eng, body):
            for i in range(LOOP_FROM):
                for g in range(G):
                    body(Slot(i // 2, i % 2, g, False))
            with eng.Fori(LOOP_FROM // 2, LOOP_TO // 2) as pair:
                for parity in range(2):
                    for g in range(G):
                        body(Slot(pair, parity, g, True))
            for i in range(LOOP_TO, LAST + 1):
                for g in range(G):
                    body(Slot(i // 2, i % 2, g, False))

        @block.sync
        def _(sp):
            sp.wait_ge(zeroed, 1)

            def load_diagonal(b, par):
                for j in range(J):
                    sp.dma_start(k_diag[j * HD:(j + 1) * HD, par, :, j * S:(j + 1) * S],
                                 k_hi_groups[b, j]).then_inc(diag_got[par], 16)

            for n in range(2):
                sp.wait_ge(k_out[n], 32 * ((NK + 1 - n) // 2))
            load_diagonal(0, 0)
            for n in range(2):
                sp.wait_ge(v_out[n], 16 * ((CT + 1 - n) // 2))

            def stack_queries(h, end, done):
                for j in range(J):
                    rows = slice(j * HD, (j + 1) * HD)
                    for part, src in enumerate((0, 1, 0)):
                        sp.dma_start(q_stack[part * HD:(part + 1) * HD, h:end, j, :],
                                     q_part[rows, h:end, src, :]).then_inc(done, 16)

            def settle(t):
                if t.steady:
                    sp.sem_inc(sp_passed, 1)

            def slot(t):
                i, s, g = t.i, t.s, t.g
                if t.has(2):
                    b, half, par, h = t.unit(2)
                    sp.wait_ge(max_rows, s - 1)
                    settle(t)
                    wait_from_first(sp, scored, s - 5)
                    sp.dma_start(q_stack[3 * HD:STACK, h, :, :], max_row[:, g % 2, :]).then_inc(max_stacked[h], 16)
                if t.has(10) and (g - 10) % 2:
                    b, half, par, j = t.unit(10)
                    sp.wait_ge(added, s - 9)
                    settle(t)
                    sp.dma_start(out_pair[b, j // 2], res[:, par, j - 1:j + 1, :]).then_inc(stored[par], 16)
                if g == 1 and t.batch_ok(3):
                    b, half, par = t.batch(3)
                    wait_from_first(sp, inp.normed, 4 * (b - 2) + 4)
                    settle(t)
                    sp.dma_start(inp.x_in[:, par, :, :], inp.x_load[b]).then_inc(inp.x_got[par], 16)
                if g == 1 and t.batch_ok(0):
                    b, half, par = t.batch(0)
                    wait_from_first(sp, v_lo, b - 1)
                    settle(t)
                    sp.dma_start(v_sb[:, par, :], v_batch[b]).then_inc(v_got[par], 16)
                    wait_from_first(sp, scored, 4 * (b - 2) + 4)
                    settle(t)
                    for part, src in enumerate((k_hi_heads, k_hi_heads, k_lo_heads)):
                        sp.dma_start(k_stack[part * HD:(part + 1) * HD, par, :, :], src[b]).then_inc(k_got[par], 16)
                if g == 3 and t.batch_ok(-1):
                    b, half, par = t.batch(-1)
                    wait_from_first(sp, stored[par], 16 * 2 * half)
                    settle(t)
                    sp.dma_start(res[:, par, :, :], inp.x_load[b]).then_inc(res_got[par], 16)
                if g == 3 and t.batch_ok(1):
                    b, half, par = t.batch(1)
                    wait_from_first(sp, max_mm, 4 * (b - 2) + 4)
                    settle(t)
                    load_diagonal(b, par)
                if g % 2 == 0 and t.has(2):
                    b, half, par, h = t.unit(2)
                    sp.wait_ge(q_lo, s)
                    settle(t)
                    wait_from_first(sp, scored, s - 4)
                    stack_queries(1 if not t.steady and s == 2 else h, h + 2, stacked[h // 2])
                elif not t.steady and s == 1:
                    sp.wait_ge(q_lo, 1)
                    stack_queries(0, 1, first_stacked)

            run(sp, slot)
            for par in range(2):
                sp.wait_ge(stored[par], 16 * 2 * B // 2)

        @block.tensor
        def _(pe):
            def slot(t):
                i, s, g = t.i, t.s, t.g
                if t.has(4):
                    b, half, par, h = t.unit(4)
                    if not t.steady and s == 4:
                        pe.wait_ge(first_stacked, 16 * 3 * J)
                    else:
                        pe.wait_ge(stacked[h // 2], 16 * 3 * J * (b + 1))
                    pe.wait_ge(max_stacked[h], 16 * (b + 1))
                    if h == 0:
                        pe.wait_ge(k_got[par], 16 * 3 * (half + 1))
                    pe.wait_ge(max_red, s - 1 if t.steady else min(s - 1, UNITS))
                    if not t.steady:
                        wait_from_first(pe, exped, s - 4)
                    for j in range(J):
                        mm = nc.tensor.matmul(score_ps[0:S, j, :], k_stack[:, par, J * h + j, :], q_stack[:, h, j, :],
                                              start=True, stop=True)
                    mm.then_inc(scored, 1)
                if t.has(0):
                    if g == 0:
                        pe.wait_ge(h_lo, 4 * i + 4)
                    if t.steady or s > PROJECT:
                        wait_from_first(pe, max_rows, s - 1)
                    else:
                        wait_from_first(pe, q_read, s)
                    if not t.steady and s > SPARE:
                        wait_from_first(pe, h_lo, min(s + 4, UNITS))
                    for k in range(KT):
                        for w, h in ((0, 0), (0, 1), (1, 0)):
                            mm = nc.tensor.matmul(a_ps[:, :], wq[:, w, k, g * P:(g + 1) * P], h_t[:, t.parity, h, k, :],
                                                  start=(k == 0 and w == 0 and h == 0), stop=(k == KT - 1 and w == 1))
                    mm.then_inc(q_done, 1)
                if t.has(6):
                    pe.wait_ge(o_full, s - 5)
                    if t.steady or s <= UNITS + 1:
                        wait_from_first(pe, added, s - 9)
                        if not t.steady and s <= PROJECT:
                            pe.wait_ge(max_rows, s - 1)
                    else:
                        pe.wait_ge(o_lo, s - 6)
                    for q in range(TT):
                        mm = nc.tensor.transpose(b_ps[:, q * P:(q + 1) * P], o_norm[:, q, :], ident)
                    mm.then_inc(o_turned, 1)
                if t.has(1):
                    b, half, par, h = t.unit(1)
                    pe.wait_ge(q_hi, s)
                    if not t.steady and s == 1:
                        pe.wait_ge(ready, READY)
                    if h == 0:
                        pe.wait_ge(diag_got[par], 16 * J * (half + 1))
                    wait_from_first(pe, exped, s - 3)
                    if not t.steady:
                        wait_from_first(pe, max_red, s - 1)
                    for q in range(TT):
                        mm = nc.tensor.matmul(score_ps[:, q, 0:J * S], q_part[:, h, 0, q * P:(q + 1) * P],
                                              k_diag[:, par, h, :], start=True, stop=True)
                    mm.then_inc(max_mm, 1)
                if t.has(5):
                    b, half, par, h = t.unit(5)
                    u = (g + 1) % 2
                    if h == 0:
                        pe.wait_ge(v_lo, b + 1)
                    pe.wait_ge(p_lo_v, s - 4)
                    pe.wait_ge(p_lo_p, s - 4)
                    if not t.steady:
                        wait_from_first(pe, o_full, s - 5)
                    for q in range(TT):
                        for j in range(J):
                            head = J * h + j
                            cell = o_heads[:, q // 2, q % 2 * J + j, :]
                            hi, lo = (p_part[:, u, part, j, q * P:(q + 1) * P] for part in range(2))
                            nc.tensor.matmul(cell, hi, v_part[:, par, head, 0:HD + 1], start=True, stop=False)
                            nc.tensor.matmul(cell[:, 0:HD], hi, v_part[:, par, head, HD + 1:2 * HD + 1],
                                             start=False, stop=False)
                            mm = nc.tensor.matmul(cell, lo, v_part[:, par, head, 0:HD + 1], start=False, stop=True)
                    mm.then_inc(valued, 1)
                if t.batch_ok(1):
                    b, half, par = t.batch(1)
                    if g == 0:
                        pe.wait_ge(inp.normed, 4 * b + 4)
                    if t.has(0) and (t.steady or s >= SPARE):
                        pe.wait_ge(q_read, s + 1)
                    if not t.steady:
                        wait_from_first(pe, h_lo, s + 4)
                    inp.turn(pe, t, turn_bank(t))
                if t.has(9):
                    b, half, par, j = t.unit(9)
                    if j == 0:
                        pe.wait_ge(o_lo, 4 * b + 4)
                    if t.steady or s <= UNITS:
                        pe.wait_ge(o_lo, s - 5)
                    elif s < UNITS + 6:
                        pe.wait_ge(max_rows, UNITS)
                        pe.wait_ge(added, s - 9)
                    else:
                        pe.wait_ge(o_lo, UNITS)
                        pe.wait_ge(added, s - 10)
                    for k in range(KT):
                        for o, w in ((0, 0), (0, 1), (1, 0)):
                            mm = nc.tensor.matmul(projection_bank(t, 0)[:, :], o_part[:, par, o, k, j * P:(j + 1) * P], wo[:, w, k, :],
                                                  start=(k == 0 and o == 0 and w == 0), stop=(k == KT - 1 and o == 1))
                    mm.then_inc(projected, 1)
                if t.has(1):
                    pe.wait_ge(max_lo, s)
                    if not t.steady and SPARE <= s < PROJECT:
                        if t.has(6):
                            pe.wait_ge(o_lo, s - 5)
                    elif t.batch_ok(1) and (t.steady or s >= SPARE):
                        pe.wait_ge(h_lo, s + 5)
                    elif t.has(0) and s >= SPARE:
                        pe.wait_ge(q_read, s + 1)
                    if not t.steady:
                        wait_from_first(pe, max_rows, s - 1)
                    nc.tensor.transpose(max_bank(t, 0)[0:2 * J * TT, 0:P], max_part[:, :, :, :].rearrange("p a j q -> p (a j q)"),
                                        ident16[:, :]).then_inc(max_t, 1)

            run(pe, slot)

        @block.scalar
        def _(act):
            def slot(t):
                i, s, g = t.i, t.s, t.g
                if t.has(2):
                    act.wait_ge(max_t, s - 1)
                    wait_from_first(act, max_stacked[g], 16 * i)
                    nc.scalar.activation(max_row[:, g % 2, :], max_bank(t, 1)[0:2 * J * TT, 0:P], ACT.Copy).then_inc(max_rows, 1)
                if t.has(1):
                    b, half, par, h = t.unit(1)
                    act.wait_ge(q_full, s)
                    wait_from_first(act, stacked[h // 2], 16 * 3 * J * b)
                    nc.scalar.activation(q_part[:, h, 0, :], q_rot[:, :], ACT.Copy).then_inc(q_hi, 1)
                if t.has(4):
                    act.wait_ge(scored, s - 3)
                    wait_from_first(act, p_lo_v, s - 5)
                    wait_from_first(act, p_lo_p, s - 5)
                    nc.scalar.activation(probs[:, g % 2, :, :], score_ps[0:S, :, :], ACT.Exp,
                                         scale=exp_scale[0:S, :]).then_inc(exped, 1)
                if t.has(-9):
                    inp.square(act, t)
                if t.has(6):
                    b, half, par, h = t.unit(6)
                    act.wait_ge(o_turned, s - 5)
                    wait_from_first(act, projected, 4 * (b - 2) + 4)
                    nc.scalar.activation(o_part[:, par, 0, h, :], b_ps[:, :], ACT.Copy).then_inc(o_hi, 1)
                if t.has(4):
                    act.wait_ge(exped, s - 3)
                    wait_from_first(act, valued, s - 5)
                    nc.scalar.activation(p_part[:, g % 2, 0, :, :], probs[:, g % 2, :, :], ACT.Copy).then_inc(p_hi, 1)
                if g == 2 and t.batch_ok(0):
                    b, half, par = t.batch(0)
                    act.wait_ge(v_got[par], 16 * (half + 1))
                    wait_from_first(act, valued, 4 * (b - 2) + 4)
                    nc.scalar.activation(v_part[:, par, :, 0:HD], v_sb[:, par, :].rearrange("s (h d) -> s h d", d=HD),
                                         ACT.Copy, scale=v_gain[0:S, :]).then_inc(v_hi, 1)
                if t.batch_ok(1):
                    inp.high(act, t, turn_bank(t))
                if t.has(-8):
                    inp.normalise(act, t)

            run(act, slot)

        @block.gpsimd
        def _(pool):
            nc.gpsimd.memset(k_stack[3 * HD:STACK, :, :, :], -1.0).then_inc(ready, 1)
            nc.gpsimd.memset(v_part[:, :, :, HD:HD + 1], 1.0).then_inc(ready, 1)
            pool.wait_ge(ready, READY)

            def slot(t):
                i, s, g = t.i, t.s, t.g
                if t.has(1):
                    b, half, par, h = t.unit(1)
                    pool.wait_ge(q_hi, s)
                    nc.gpsimd.tensor_tensor(q_part[:, h, 1, :], q_rot[:, :], q_part[:, h, 0, :],
                                            ALU.subtract).then_inc(q_lo, 1)
                if t.has(-9):
                    inp.root(pool, t)
                if t.has(0):
                    pool.wait_ge(q_read, s + 1)
                    wait_from_first(pool, q_full, s)
                    nc.gpsimd.tensor_tensor(sin_part[:, :], swapped[:, :], sin_q, ALU.mult).then_inc(q_sin, 1)
                if t.has(4):
                    pool.wait_ge(p_hi, s - 3)
                    nc.gpsimd.tensor_tensor(p_part[:, g % 2, 1, LO_V:J, :], probs[:, g % 2, LO_V:J, :],
                                            p_part[:, g % 2, 0, LO_V:J, :], ALU.subtract).then_inc(p_lo_p, 1)

            run(pool, slot)

        @block.vector
        def _(dve):
            nc.vector.memset(k_diag[:, :, :, :], 0.0).then_inc(zeroed, 1)
            nc.vector.tensor_copy(ident16[:, :], ident).then_inc(ready, 1)

            def slot(t):
                i, s, g = t.i, t.s, t.g
                if t.has(1):
                    dve.wait_ge(q_sin, s)
                    dve.wait_ge(q_read, s)
                    wait_from_first(dve, q_lo, s - 1)
                    nc.vector.tensor_tensor(q_rot[:, :], cos_part[:, :], sin_part[:, :], ALU.add).then_inc(q_full, 1)

                def output():
                    if t.has(10):
                        b, half, par, j = t.unit(10)
                        dve.wait_ge(projected, s - 9)
                        dve.wait_ge(res_got[par], 16 * (half + 1))
                        nc.vector.scalar_tensor_tensor(out=res[:, par, j, :], in0=projection_bank(t, 1)[:, :],
                                                       scalar=out_scale, in1=res[:, par, j, :],
                                                       op0=ALU.mult, op1=ALU.add).then_inc(added, 1)

                def divide():
                    if t.has(6):
                        dve.wait_ge(valued, s - 5)
                        wait_from_first(dve, o_full, s - 6)
                        nc.vector.reciprocal(recip[:, :].rearrange("p (b n) -> p b n", b=2),
                                             o_heads[:, :, :, HD]).then_inc(recip_done, 1)
                        dve.wait_ge(recip_done, s - 5)
                        wait_from_first(dve, o_turned, s - 6)
                        nc.vector.tensor_tensor(
                            o_norm[:, :, :].rearrange("p (b q) (j c) -> p b (q j) c", b=2, c=HD), o_heads[:, :, :, 0:HD],
                            recip[:, :].rearrange("p (b n) -> p b n", b=2).unsqueeze(3).to_broadcast([P, 2, TT * J // 2, HD]),
                            ALU.mult).then_inc(o_full, 1)

                for stage in (output, divide) if t.steady or s <= UNITS + 1 else (divide, output):
                    stage()
                if t.has(5):
                    u = (g + 1) % 2
                    dve.wait_ge(p_hi, s - 4)
                    nc.vector.tensor_tensor(p_part[:, u, 1, 0:LO_V, :], probs[:, u, 0:LO_V, :], p_part[:, u, 0, 0:LO_V, :],
                                            ALU.subtract).then_inc(p_lo_v, 1)
                if t.has(0):
                    dve.wait_ge(q_done, s + 1)
                    wait_from_first(dve, q_sin, s)
                    wait_from_first(dve, q_full, s)
                    nc.vector.tensor_tensor(cos_part[:, :], a_ps[:, :], cos_q, ALU.mult)
                    nc.vector.stream_shuffle(swapped[:, :], a_ps[:, :], SWAP).then_inc(q_read, 1)
                if t.has(6):
                    b, half, par, h = t.unit(6)
                    dve.wait_ge(o_hi, s - 5)
                    nc.vector.tensor_tensor(o_part[:, par, 1, h, :], b_ps[:, :], o_part[:, par, 0, h, :],
                                            ALU.subtract).then_inc(o_lo, 1)
                if t.has(1):
                    dve.wait_ge(max_mm, s)
                    wait_from_first(dve, max_lo, s - 1)
                    nc.vector.tensor_reduce(maxima[:, :, :].rearrange("p j q -> p q j"),
                                            score_ps[:, :, 0:J * S].rearrange("p q (j k) -> p q j k", k=S), AX.X, ALU.max).then_inc(max_red, 1)
                    dve.wait_ge(max_red, s)
                    wait_from_first(dve, max_t, s - 1)
                    nc.vector.tensor_copy(max_part[:, 0, :, :], maxima[:, :, :]).then_inc(max_hi, 1)
                    dve.wait_ge(max_hi, s)
                    nc.vector.tensor_tensor(max_part[:, 1, :, :], maxima[:, :, :], max_part[:, 0, :, :],
                                            ALU.subtract).then_inc(max_lo, 1)
                if g == 2 and t.batch_ok(0):
                    b, half, par = t.batch(0)
                    dve.wait_ge(v_hi, b + 1)
                    nc.vector.scalar_tensor_tensor(
                        out=v_part[:, par, :, HD + 1:2 * HD + 1], in0=v_sb[:, par, :].rearrange("s (h d) -> s h d", d=HD),
                        scalar=v_gain[0:S, :], in1=v_part[:, par, :, 0:HD], op0=ALU.mult, op1=ALU.subtract).then_inc(v_lo, 1)
                if t.batch_ok(1):
                    inp.low(dve, t, turn_bank(t))

            run(dve, slot)


def cross_attention(nc, x, ctx_in, norm_w, w_q, w_kv, w_o, consts_in, out):
    with ExitStack() as ctx:
        sb = lambda name, shape, dt: ctx.enter_context(nc.sbuf_tensor(name, shape, dt))
        k_hi_dram = nc.dram_tensor("k_hi_dram", [D, NTOK], F16, kind="Internal").ap()
        k_lo_dram = nc.dram_tensor("k_lo_dram", [D, NTOK], F16, kind="Internal").ap()
        v_dram = nc.dram_tensor("v_dram", [NTOK, D], F32, kind="Internal").ap()
        keep = (
            sb("consts", [P, C_END], F32),
            sb("wq", [P, 2, KT, D], F16),
            sb("wo", [P, 2, KT, D], F16),
            sb("scales", [P, 4], F32),
        )
        stores = (
            sb("k_part", [P, 2, 2, KCHUNK], F16),
            sb("v_row", [P, 2, D], F32),
            [ctx.enter_context(nc.semaphore(f"k_out{n}")) for n in range(2)],
            [ctx.enter_context(nc.semaphore(f"v_out{n}")) for n in range(2)],
        )
        inp = Input(nc, ctx, x, keep[0][:, C_ID:C_ID + P])
        setup_block(nc, keep, stores, inp, ctx_in.rearrange("b s d -> (b s) d"), norm_w, w_q, w_kv, w_o, consts_in,
                    k_hi_dram, k_lo_dram, v_dram)
        attention_block(nc, keep, stores, inp, x, out, k_hi_dram, k_lo_dram, v_dram)


def kernel(x, ctx_1024, L0_xattn_norm_w, L0_xattn_Wq, L0_xattn_Wkv, L0_xattn_Wo):
    import numpy as np
    import concourse.bacc as bacc
    from concourse.bass_utils import run_bass_kernel_spmd

    nc = bacc.Bacc("TRN2", target_bir_lowering=False, num_devices=1)
    arrays = {
        "x": np.ascontiguousarray(x), "ctx": np.ascontiguousarray(ctx_1024),
        "norm_w": np.ascontiguousarray(L0_xattn_norm_w), "w_q": np.ascontiguousarray(L0_xattn_Wq),
        "w_kv": np.ascontiguousarray(L0_xattn_Wkv), "w_o": np.ascontiguousarray(L0_xattn_Wo),
        "shape_constants": shape_constants(),
    }
    aps = [nc.dram_tensor(name, a.shape, mybir.dt.from_np(a.dtype), kind="ExternalInput").ap()
           for name, a in arrays.items()]
    out = nc.dram_tensor("out", (B, T, D), F32, kind="ExternalOutput").ap()
    cross_attention(nc, *aps, out)
    return run_bass_kernel_spmd(nc, [arrays], core_ids=[0]).results[0]["out"]
```
